# Optimizing a Trainium2 kernel written in Bass

```python
import numpy as np
import jax
import jax.numpy as jnp

def _softmax(x, axis=-1):
    return jax.nn.softmax(x, axis=axis)

def _gelu(x):
    return jax.nn.gelu(x, approximate=True)

def _silu(x):
    return jax.nn.silu(x)

def _sigmoid(x):
    return jax.nn.sigmoid(x)

def _layernorm(x, axis=-1, eps=1e-05):
    m = jnp.mean(x, axis=axis, keepdims=True)
    v = jnp.var(x, axis=axis, keepdims=True)
    return (x - m) / jnp.sqrt(v + eps)

def _scatter_add(tgt, idx, src, axis=0):
    return tgt.at[idx].add(src)

def _segment_sum(src, seg, n):
    return jax.ops.segment_sum(src, seg, n)
kernel_name = 'mk_seq_postln_d1_jaxref_r4_740e70'

def setup_inputs(seed: int=0):
    np.random.seed(seed)
    _w = jnp.asarray

    def _L0_attn_setup():
        import jax, jax.numpy as jnp
        import numpy as np
        import math
        N, S, E, H = (4, 1024, 256, 16)
        D = E // H
        key = jax.random.key(seed)
        ks = jax.random.split(key, 9)
        w = 1.0 / math.sqrt(E)
        mk = lambda k, shape: jax.random.normal(k, shape, jnp.float32) * w
        return {'x': jax.random.normal(ks[0], (N, S, E), jnp.float32), 'Wq': mk(ks[1], (E, E)), 'bq': mk(ks[2], (E,)), 'Wk': mk(ks[3], (E, E)), 'bk': mk(ks[4], (E,)), 'Wv': mk(ks[5], (E, E)), 'bv': mk(ks[6], (E,)), 'Wo': mk(ks[7], (E, E)), 'bo': mk(ks[8], (E,))}
    _L0_attn_in = _L0_attn_setup()

    def _L0_ffn_setup():
        import jax, jax.numpy as jnp
        import numpy as np
        DIM = 256

        def _reference_tuple_inner(x, W_r, W_k, W_v, mu_r, mu_k):
            B, T, C = x.shape
            x_prev = jnp.concatenate([jnp.zeros((B, 1, C), x.dtype), x[:, :-1, :]], axis=1)
            xr = mu_r * x + (1.0 - mu_r) * x_prev
            xk = mu_k * x + (1.0 - mu_k) * x_prev
            r = jax.nn.sigmoid(jnp.einsum('btc,dc->btd', xr, W_r))
            k = jnp.einsum('btc,dc->btd', xk, W_k)
            k_act = jnp.square(jax.nn.relu(k))
            out = r * jnp.einsum('btc,dc->btd', k_act, W_v)
            new_state = x[:, -1, :]
            return (out, new_state)
        key = jax.random.key(seed)
        ks = jax.random.split(key, 6)
        B, T, C = (8, 512, DIM)
        x = jax.random.normal(ks[0], (B, T, C), dtype=jnp.float32)
        s = 1.0 / np.sqrt(C)
        W_r = jax.random.uniform(ks[1], (C, C), jnp.float32, -s, s)
        W_k = jax.random.uniform(ks[2], (C, C), jnp.float32, -s, s)
        W_v = jax.random.uniform(ks[3], (C, C), jnp.float32, -s, s)
        mu_r = jax.random.uniform(ks[4], (C,), jnp.float32)
        mu_k = jax.random.uniform(ks[5], (C,), jnp.float32)
        return {'x': x, 'W_r': W_r, 'W_k': W_k, 'W_v': W_v, 'mu_r': mu_r, 'mu_k': mu_k}
    _L0_ffn_in = _L0_ffn_setup()
    _d = {'L0_attn_x': _L0_attn_in['x'], 'L0_attn_Wq': _L0_attn_in['Wq'], 'L0_attn_bq': _L0_attn_in['bq'], 'L0_attn_Wk': _L0_attn_in['Wk'], 'L0_attn_bk': _L0_attn_in['bk'], 'L0_attn_Wv': _L0_attn_in['Wv'], 'L0_attn_bv': _L0_attn_in['bv'], 'L0_attn_Wo': _L0_attn_in['Wo'], 'L0_attn_bo': _L0_attn_in['bo'], 'L0_ffn_W_r': _L0_ffn_in['W_r'], 'L0_ffn_W_k': _L0_ffn_in['W_k'], 'L0_ffn_W_v': _L0_ffn_in['W_v'], 'L0_ffn_mu_r': _L0_ffn_in['mu_r'], 'L0_ffn_mu_k': _L0_ffn_in['mu_k']}
    _x0 = _d['L0_attn_x']
    _d['L0_attn_x'] = jax.random.normal(jax.random.fold_in(jax.random.key(seed), 1), (4, 2048, 256), dtype=_x0.dtype)
    del _x0
    return _d

def reference(L0_attn_x, L0_attn_Wq, L0_attn_bq, L0_attn_Wk, L0_attn_bk, L0_attn_Wv, L0_attn_bv, L0_attn_Wo, L0_attn_bo, L0_ffn_W_r, L0_ffn_W_k, L0_ffn_W_v, L0_ffn_mu_r, L0_ffn_mu_k):

    def _L0_attn_ref(x, Wq, bq, Wk, bk, Wv, bv, Wo, bo):
        import jax, jax.numpy as jnp
        import numpy as np
        import math
        N, S, E, H = (4, 1024, 256, 16)
        D = E // H
        n, s, e = x.shape
        h, d = (H, D)
        scale = 1.0 / math.sqrt(d)

        def proj(W, b):
            y = jnp.einsum('nse,fe->nsf', x, W) + b
            return y.reshape(n, s, h, d).transpose(0, 2, 1, 3)
        Q = proj(Wq, bq)
        K = proj(Wk, bk)
        V = proj(Wv, bv)
        scores = jnp.einsum('nqhd,nkhd->nhqk', Q, K) * scale
        attn = jax.nn.softmax(scores, axis=-1)
        out = jnp.einsum('nhql,nlhd->nqhd', attn, V)
        out = out.reshape(n, s, e)
        return jnp.einsum('nse,fe->nsf', out, Wo) + bo

    def _L0_ffn_ref(x, W_r, W_k, W_v, mu_r, mu_k):
        import jax, jax.numpy as jnp
        import numpy as np
        DIM = 256

        def _reference_tuple_inner(x, W_r, W_k, W_v, mu_r, mu_k):
            B, T, C = x.shape
            x_prev = jnp.concatenate([jnp.zeros((B, 1, C), x.dtype), x[:, :-1, :]], axis=1)
            xr = mu_r * x + (1.0 - mu_r) * x_prev
            xk = mu_k * x + (1.0 - mu_k) * x_prev
            r = jax.nn.sigmoid(jnp.einsum('btc,dc->btd', xr, W_r))
            k = jnp.einsum('btc,dc->btd', xk, W_k)
            k_act = jnp.square(jax.nn.relu(k))
            out = r * jnp.einsum('btc,dc->btd', k_act, W_v)
            new_state = x[:, -1, :]
            return (out, new_state)
        return _reference_tuple_inner(x, W_r, W_k, W_v, mu_r, mu_k)[0]
    x = L0_attn_x
    x = _layernorm(x + _L0_attn_ref(x, L0_attn_Wq, L0_attn_bq, L0_attn_Wk, L0_attn_bk, L0_attn_Wv, L0_attn_bv, L0_attn_Wo, L0_attn_bo), axis=-1)
    x = _layernorm(x + _L0_ffn_ref(x, L0_ffn_W_r, L0_ffn_W_k, L0_ffn_W_v, L0_ffn_mu_r, L0_ffn_mu_k), axis=-1)
    return x

_drawn_inputs = setup_inputs


def setup_inputs(seed=0):
    import zlib

    import numpy as np

    out = dict(_drawn_inputs(seed))
    spreads = {}
    factors = {'L0_attn_bq': 3.104, 'L0_attn_bk': 3.17, 'L0_ffn_W_r': 3.186, 'L0_ffn_mu_r': 6.419}
    for name, (base, spread) in spreads.items():
        noise = np.random.default_rng([zlib.crc32(name.encode()), seed]).standard_normal(out[name].shape)
        drawn = base * np.exp(spread * noise) if base else spread * noise
        out[name] = jnp.asarray(drawn.astype(out[name].dtype))
    for name, factor in factors.items():
        out[name] = (out[name] * factor).astype(out[name].dtype)
    return out
```

```python
from contextlib import ExitStack

import concourse.bass as bass
from concourse import mybir

ALU = mybir.AluOpType
ACT = mybir.ActivationFunctionType
AX = mybir.AxisListType
F32 = mybir.dt.float32
ds = bass.ds

P = 128
BATCH, SEQ, E, HEADS = 4, 2048, 256, 16
D = E // HEADS
ECH = E // P
SLICE = 2 * P
SLICES = BATCH * SEQ // SLICE
PER_BATCH = SEQ // SLICE
LAG = PER_BATCH
HALF = HEADS // 2
SCALE = float(D) ** -0.5
EPS = 1e-5
DMA = 16


def build(nc, x_tok, x_t, wqk_t, wv_t, wo_t, wr_t, wkk_t, wvv_t, bqk, bv, bo, mu_r, mu_k, out):
    heads_out = nc.dram_tensor("heads_out", [BATCH + 1, HEADS, SEQ, D], F32).ap()

    with ExitStack() as ctx:
        def sb(name, shape, dt=F32):
            return ctx.enter_context(nc.sbuf_tensor(name, shape, dt))

        def ps(name):
            return ctx.enter_context(nc.psum_tensor(name, [P, 512], F32))

        def sem(name):
            return ctx.enter_context(nc.semaphore(name))

        w_dram = {"wqk": wqk_t, "wv": wv_t, "wo": wo_t, "wr": wr_t, "wkk": wkk_t, "wvv": wvv_t}
        w = {n: sb(n + "_sb", [P, ECH, a.shape[1]]) for n, a in w_dram.items()}
        mu = sb("mu", [P, 2, ECH])
        b_row = sb("b_row", [1, 4 * E])
        ones = sb("ones", [1, P])
        ident = sb("ident", [P, P])
        minus_half = sb("minus_half", [P, 2])
        credit = sb("credit", [P, 5])

        xt = sb("xt", [P, ECH, SLICE])
        qk = [sb(f"qk{i}", [P, 2, HEADS, D]) for i in range(2)]
        v = [sb(f"v{i}", [P, HEADS, D]) for i in range(2)]
        prod = [sb(f"prod{i}", [P, HEADS, HEADS, D]) for i in range(2)]
        scores = [sb(f"scores{i}", [P, HEADS, HEADS]) for i in range(2)]
        row_max = [sb(f"row_max{i}", [P, HEADS]) for i in range(2)]
        shifted = [sb(f"shifted{i}", [P, HEADS, HEADS]) for i in range(2)]
        probs = [sb(f"probs{i}", [P, HEADS, HEADS]) for i in range(2)]
        row_sum = [sb(f"row_sum{i}", [P, HEADS]) for i in range(2)]
        inv_sum = [sb(f"inv_sum{i}", [P, HEADS]) for i in range(2)]
        raw = [sb(f"raw{i}", [P, HEADS, D]) for i in range(2)]
        attn = [sb(f"attn{i}", [P, HEADS, D]) for i in range(2)]

        yrow = sb("yrow", [P, 2, E])
        attn_t = sb("attn_t", [P, ECH, SLICE])
        xrow = sb("xrow", [P, 2, E])
        z = sb("z", [P, 2, E])
        stats = sb("stats", [P, 2, 6])
        mean_var = sb("mean_var", [P, 2, 2])
        var_eps = sb("var_eps", [P, 2])
        rstd = sb("rstd", [P, 2])
        x1 = sb("x1", [P, 2, E])
        x1_t = sb("x1_t", [P, ECH, 1 + SLICE])
        carry = sb("carry", [P, ECH, PER_BATCH + 1])
        diff = sb("diff", [P, ECH, SLICE])
        xr = sb("xr", [P, ECH, SLICE])
        xk = sb("xk", [P, ECH, SLICE])
        gate_tanh = sb("gate_tanh", [P, 2, E])
        k_relu = sb("k_relu", [P, ECH, SLICE])
        k_act = sb("k_act", [P, ECH, SLICE])
        gated = sb("gated", [P, 2, E])
        z2 = sb("z2", [P, 2, E])
        stats2 = sb("stats2", [P, 2, 6])
        mean_var2 = sb("mean_var2", [P, 2, 2])
        var_eps2 = sb("var_eps2", [P, 2])
        rstd2 = sb("rstd2", [P, 2])
        y = sb("y", [P, 2, E])

        qk_ps, v_ps, yt_ps, o_ps, xt_ps, r_ps, kk_ps, vv_ps = (
            ps(n) for n in ("qk_ps", "v_ps", "yt_ps", "o_ps", "xt_ps", "r_ps", "kk_ps", "vv_ps"))

        consts_loaded, ident_zero, consts_ready = sem("consts_loaded"), sem("ident_zero"), sem("consts_ready")
        x_loaded = sem("x_loaded")
        qk_ready, qk_taken = sem("qk_ready"), sem("qk_taken")
        v_ready, v_taken = sem("v_ready"), sem("v_taken")
        sprod_low, sprod_high, scores_step = sem("sprod_low"), sem("sprod_high"), sem("scores_step")
        exp_done, sums_step = sem("exp_done"), sem("sums_step")
        vprod_low, vprod_high, raw_done, attn_done = sem("vprod_low"), sem("vprod_high"), sem("raw_done"), sem("attn_done")
        attn_stored = [sem(f"attn_stored{i}") for i in range(2)]
        y_loaded, x_rows_loaded = sem("y_loaded"), sem("x_rows_loaded")
        yt_ready, yt_taken, o_ready, z_ready = sem("yt_ready"), sem("yt_taken"), sem("o_ready"), sem("z_ready")
        ln1_step, ln1_rstd, x1_ready = sem("ln1_step"), sem("ln1_rstd"), sem("x1_ready")
        xt_ready, xt_taken, carry_ready = sem("xt_ready"), sem("xt_taken"), sem("carry_ready")
        diff_ready, mix_ready = sem("diff_ready"), sem("mix_ready")
        r_ready, r_taken, kk_ready, kk_taken = sem("r_ready"), sem("r_taken"), sem("kk_ready"), sem("kk_taken")
        kact_ready, vv_ready, vv_taken, z2_ready = sem("kact_ready"), sem("vv_ready"), sem("vv_taken"), sem("z2_ready")
        ln2_step, ln2_rstd, y_ready, y_stored = sem("ln2_step"), sem("ln2_rstd"), sem("y_ready"), sem("y_stored")

        N_CONST_DMAS = 6 + 2 + 3
        block = ctx.enter_context(nc.Block())

        def loops(engine, pair):
            with engine.Fori(0, LAG) as g:
                pair(g, True, False)
            with engine.Fori(LAG, SLICES - 1) as g:
                pair(g, True, True)
            pair(SLICES - 1, False, True)

        @block.sync
        def _(sp):
            def load_x(a):
                sp.dma_start(xt[:, :, :], x_t.rearrange("(c p) n -> p c n", p=P)[:, :, ds(a * SLICE, SLICE)]
                             ).then_inc(x_loaded, DMA)

            def load_finish(c):
                rows = heads_out[c >> 3].rearrange("h s d -> (h s d)").rearrange("(r f) -> r f", f=E)
                sp.dma_start(yrow[:, :, :], rows[ds((c & 7) * SLICE, SLICE), :].rearrange("(t p) f -> p t f", p=P)
                             ).then_inc(y_loaded, DMA)

            def load_x_rows(c):
                sp.dma_start(xrow[:, :, :], x_tok[ds(c * SLICE, SLICE), :].rearrange("(t p) f -> p t f", p=P)
                             ).then_inc(x_rows_loaded, DMA)

            def store_y(c):
                sp.wait_ge(y_ready, 2 * (c + 1))
                sp.dma_start(out[ds(c * SLICE, SLICE), :].rearrange("(t p) f -> p t f", p=P), y[:, :, :]
                             ).then_inc(y_stored, DMA)

            load_x(0)
            for n, a in w_dram.items():
                sp.dma_start(w[n][:, :, :], a.rearrange("(c p) f -> p c f", p=P)).then_inc(consts_loaded, DMA)
            for i, a in enumerate((mu_r, mu_k)):
                sp.dma_start(mu[:, i, :], a).then_inc(consts_loaded, DMA)
            for dst, a in ((b_row[:, 0:2 * E], bqk), (b_row[:, 2 * E:3 * E], bv), (b_row[:, 3 * E:4 * E], bo)):
                sp.dma_start(dst, a.rearrange("(o f) -> o f", o=1)).then_inc(consts_loaded, DMA)

            def pair(g, ahead, finishes):
                if ahead:
                    sp.wait_ge(v_ready, 2 * (g + 1))
                    load_x(g + 1)
                if finishes:
                    c = g - LAG
                    sp.wait_ge(z_ready, c + 1)
                    load_x_rows(c)
                    for i in range(2):
                        sp.wait_ge(attn_stored[i], (g + 1) * DMA)
                    load_finish(c)
                for i in range(2):
                    u = 2 * g + i
                    sp.wait_ge(attn_done, u + 1)
                    sp.dma_start(heads_out[g >> 3, :, ds((g & 7) * SLICE + i * P, P), :].rearrange("h s d -> s h d"),
                                 attn[i][:, :, :]).then_inc(attn_stored[i], DMA)
                if finishes:
                    store_y(g - LAG)

            loops(sp, pair)
            for i in range(2):
                sp.wait_ge(attn_stored[i], (SLICES + 1) * DMA)
            with sp.Fori(SLICES - LAG, SLICES) as c:
                sp.wait_ge(z_ready, c + 1)
                load_x_rows(c)
                load_finish(c)
                store_y(c)
            sp.wait_ge(y_stored, DMA * (SLICES + 1))

        @block.tensor
        def _(pe):
            def rows_by(dst, lhs, i, name, bias, ready=None):
                for c in range(ECH):
                    mm = nc.tensor.matmul(dst, lhs[:, c, i * P:(i + 1) * P], w[name][:, c, :],
                                          start=(c == 0), stop=(bias is None and c == ECH - 1))
                if bias is not None:
                    mm = nc.tensor.matmul(dst, ones[:, :], bias, start=False, stop=True)
                if ready is not None:
                    mm.then_inc(ready, 1)

            def project(a, i, first=False):
                u = 2 * a + i
                if i == 0:
                    pe.wait_ge(x_loaded, (a + 1) * DMA)
                if not first:
                    pe.wait_ge(qk_taken, 2 * u)
                rows_by(qk_ps[:, :], xt, i, "wqk", b_row[:, 0:2 * E], qk_ready)
                if not first:
                    pe.wait_ge(v_taken, u)
                rows_by(v_ps[:, 0:E], xt, i, "wv", b_row[:, 2 * E:3 * E], v_ready)

            def to_columns(dst, src, ready):
                for ch in range(ECH):
                    for t in range(2):
                        mm = nc.tensor.transpose(dst[:, ch * SLICE + t * P:ch * SLICE + (t + 1) * P],
                                                 src[:, t, ch * P:(ch + 1) * P], ident[:, :])
                mm.then_inc(ready, 1)

            def project_o(c):
                pe.wait_ge(y_loaded, (c + 1) * DMA)
                to_columns(yt_ps, yrow, yt_ready)
                pe.wait_ge(yt_taken, c + 1)
                for i in range(2):
                    rows_by(o_ps[:, i * E:(i + 1) * E], attn_t, i, "wo", b_row[:, 3 * E:4 * E], o_ready if i else None)

            def project_rk(c):
                pe.wait_ge(x1_ready, 2 * (c + 1))
                to_columns(xt_ps, x1, xt_ready)
                pe.wait_ge(mix_ready, 4 * c + 2)
                for i in range(2):
                    rows_by(r_ps[:, i * E:(i + 1) * E], xr, i, "wr", None, r_ready if i else None)
                pe.wait_ge(mix_ready, 4 * c + 4)
                for f in range(ECH):
                    for ch in range(ECH):
                        mm = nc.tensor.matmul(kk_ps[:, f * SLICE:(f + 1) * SLICE], w["wkk"][:, ch, f * P:(f + 1) * P],
                                              xk[:, ch, :], start=(ch == 0), stop=(ch == ECH - 1))
                mm.then_inc(kk_ready, 1)

            def project_vv(c):
                pe.wait_ge(kact_ready, c + 1)
                for i in range(2):
                    rows_by(vv_ps[:, i * E:(i + 1) * E], k_act, i, "wvv", None, vv_ready if i else None)

            pe.wait_ge(consts_loaded, N_CONST_DMAS * DMA)
            pe.wait_ge(consts_ready, 3)
            project(0, 0, first=True)
            project(0, 1)

            def pair(g, ahead, finishes):
                if finishes:
                    project_o(g - LAG)
                if ahead:
                    project(g + 1, 0)
                if finishes:
                    project_rk(g - LAG)
                if ahead:
                    project(g + 1, 1)
                if finishes:
                    project_vv(g - LAG)

            loops(pe, pair)
            with pe.Fori(SLICES - LAG, SLICES) as c:
                project_o(c)
                project_rk(c)
                project_vv(c)

        @block.scalar
        def _(act):
            def take_tile(a, i, first):
                u = 2 * a + i
                act.wait_ge(qk_ready, u + 1)
                if not first:
                    act.wait_ge(sprod_low, u - 1)
                    act.wait_ge(sprod_high, u - 1)
                for j, scale in ((0, SCALE), (1, 1.0)):
                    nc.scalar.activation(qk[i][:, j, :, :].rearrange("p h d -> p (h d)"), qk_ps[:, j * E:(j + 1) * E],
                                         ACT.Copy, scale=scale).then_inc(qk_taken, 1)
                act.wait_ge(v_ready, u + 1)
                if not first:
                    act.wait_ge(vprod_low, u - 1)
                    act.wait_ge(vprod_high, u - 1)
                nc.scalar.activation(v[i][:, :, :].rearrange("p h d -> p (h d)"), v_ps[:, 0:E], ACT.Copy
                                     ).then_inc(v_taken, 1)

            def exp(g, i):
                u = 2 * g + i
                act.wait_ge(scores_step, 3 * u + 3)
                nc.scalar.activation(probs[i][:, :, :], shifted[i][:, :, :], ACT.Exp).then_inc(exp_done, 1)

            def take_yt(c):
                act.wait_ge(yt_ready, c + 1)
                nc.scalar.activation(attn_t[:, :, :].rearrange("p c n -> p (c n)"), yt_ps[:, :], ACT.Copy
                                     ).then_inc(yt_taken, 1)

            def take_x1_t(c):
                act.wait_ge(xt_ready, c + 1)
                act.wait_ge(carry_ready, c + 1)
                nc.scalar.activation(x1_t[:, :, 1:1 + SLICE], xt_ps[:, :].rearrange("p (c n) -> p c n", c=ECH), ACT.Copy
                                     ).then_inc(xt_taken, 1)

            def take_rk(c):
                act.wait_ge(r_ready, c + 1)
                nc.scalar.activation(gate_tanh[:, :, :].rearrange("p t f -> p (t f)"), r_ps[:, :], ACT.Tanh, scale=0.5
                                     ).then_inc(r_taken, 1)
                act.wait_ge(kk_ready, c + 1)
                nc.scalar.activation(k_relu[:, :, :].rearrange("p c n -> p (c n)"), kk_ps[:, :], ACT.Relu
                                     ).then_inc(kk_taken, 1)

            take_tile(0, 0, True)
            take_tile(0, 1, True)

            def pair(g, ahead, finishes):
                if finishes:
                    take_yt(g - LAG)
                exp(g, 0)
                exp(g, 1)
                if finishes:
                    take_x1_t(g - LAG)
                if ahead:
                    take_tile(g + 1, 0, False)
                if finishes:
                    take_rk(g - LAG)
                if ahead:
                    take_tile(g + 1, 1, False)

            loops(act, pair)
            with act.Fori(SLICES - LAG, SLICES) as c:
                take_yt(c)
                take_x1_t(c)
                take_rk(c)

        def score_product(engine, i, lo, hi):
            n = hi - lo
            q = qk[i][:, 0, lo:hi, :].rearrange("p (q o) d -> p q o d", o=1).broadcast_to([P, n, HEADS, D])
            k = qk[i][:, 1, :, :].rearrange("p (o k) d -> p o k d", o=1).broadcast_to([P, n, HEADS, D])
            return engine.tensor_tensor(prod[i][:, lo:hi, :, :], q, k, ALU.mult)

        def value_product(engine, i, lo, hi):
            n = hi - lo
            pr = probs[i][:, lo:hi, :].rearrange("p q (o k) -> p q o k", o=1).broadcast_to([P, n, D, HEADS])
            vv = v[i][:, :, :].rearrange("p (o k) d -> p o d k", o=1).broadcast_to([P, n, D, HEADS])
            return engine.tensor_tensor(prod[i][:, lo:hi, :, :], pr, vv, ALU.mult)

        @block.vector
        def _(dve):
            def score(g, i):
                u = 2 * g + i
                dve.wait_ge(qk_taken, 2 * (u + 1))
                score_product(nc.vector, i, 0, HEADS - HALF).then_inc(sprod_low, 1)
                dve.wait_ge(sprod_high, u + 1)
                dve.wait_ge(sprod_low, u + 1)
                nc.vector.tensor_reduce(scores[i][:, :, :], prod[i][:, :, :, :], AX.X, ALU.add).then_inc(scores_step, 1)
                dve.wait_ge(scores_step, 3 * u + 1)
                nc.vector.tensor_reduce(row_max[i][:, :], scores[i][:, :, :], AX.X, ALU.max).then_inc(scores_step, 1)
                dve.wait_ge(scores_step, 3 * u + 2)
                m = row_max[i][:, :].rearrange("p (q o) -> p q o", o=1).broadcast_to([P, HEADS, HEADS])
                nc.vector.tensor_tensor(shifted[i][:, :, :], scores[i][:, :, :], m, ALU.subtract).then_inc(scores_step, 1)

            def weigh(g, i):
                u = 2 * g + i
                dve.wait_ge(v_taken, u + 1)
                dve.wait_ge(exp_done, u + 1)
                value_product(nc.vector, i, 0, HEADS - HALF).then_inc(vprod_low, 1)
                nc.vector.tensor_reduce(row_sum[i][:, :], probs[i][:, :, :], AX.X, ALU.add).then_inc(sums_step, 1)
                dve.wait_ge(sums_step, 2 * u + 1)
                nc.vector.reciprocal(inv_sum[i][:, :], row_sum[i][:, :]).then_inc(sums_step, 1)
                dve.wait_ge(vprod_high, u + 1)
                dve.wait_ge(vprod_low, u + 1)
                nc.vector.tensor_reduce(raw[i][:, :, :], prod[i][:, :, :, :], AX.X, ALU.add).then_inc(raw_done, 1)
                dve.wait_ge(raw_done, u + 3)
                dve.wait_ge(sums_step, 2 * u + 2)
                inv = inv_sum[i][:, :].rearrange("p (q o) -> p q o", o=1).broadcast_to([P, HEADS, D])
                dve.wait_ge(attn_stored[i], (g + 1) * DMA)
                nc.vector.tensor_tensor(attn[i][:, :, :], raw[i][:, :, :], inv, ALU.mult).then_inc(attn_done, 1)

            def moments(src, stats_t, mv, ve, step, c):
                for t in range(2):
                    nc.vector.bn_stats(stats_t[:, t, :], src[:, t, :]).then_inc(step, 1)
                dve.wait_ge(step, c * 5 + 2)
                nc.vector.memset(ve[:, :], 0.0)
                for t in range(2):
                    nc.vector.bn_aggr(mv[:, t, :], stats_t[:, t, :]).then_inc(step, 1)
                dve.wait_ge(step, c * 5 + 4)
                nc.vector.tensor_scalar(ve[:, :], mv[:, :, 1], EPS, None, ALU.add).then_inc(step, 1)

            def take_o(c):
                dve.wait_ge(x_rows_loaded, (c + 1) * DMA)
                dve.wait_ge(o_ready, c + 1)
                nc.vector.tensor_tensor(z[:, :, :].rearrange("p t f -> p (t f)"), o_ps[:, :],
                                        xrow[:, :, :].rearrange("p t f -> p (t f)"), ALU.add).then_inc(z_ready, 1)
                dve.wait_ge(z_ready, c + 2)
                moments(z, stats, mean_var, var_eps, ln1_step, c)

            def normalise(src, mv, rs, dst, rstd_ready, ready, c):
                dve.wait_ge(rstd_ready, c + 1)
                for t in range(2):
                    nc.vector.tensor_scalar(dst[:, t, :], src[:, t, :], mv[:, t, 0:1], rs[:, t:t + 1],
                                            ALU.subtract, ALU.mult).then_inc(ready, 1)

            def mix(c):
                dve.wait_ge(diff_ready, c + 1)
                for i, dst in enumerate((xr, xk)):
                    for ch in range(ECH):
                        nc.vector.scalar_tensor_tensor(out=dst[:, ch, :], in0=diff[:, ch, :], scalar=mu[:, i, ch:ch + 1],
                                                       in1=x1_t[:, ch, 0:SLICE], op0=ALU.mult, op1=ALU.add
                                                       ).then_inc(mix_ready, 1)

            def take_vv(c):
                dve.wait_ge(vv_ready, c + 1)
                dve.wait_ge(r_taken, c + 1)
                nc.vector.scalar_tensor_tensor(out=gated[:, :, :].rearrange("p t f -> p (t f)"),
                                               in0=gate_tanh[:, :, :].rearrange("p t f -> p (t f)"), scalar=1.0,
                                               in1=vv_ps[:, :], op0=ALU.add, op1=ALU.mult).then_inc(vv_taken, 1)
                dve.wait_ge(vv_taken, c + 1)
                nc.vector.tensor_tensor(z2[:, :, :], gated[:, :, :], x1[:, :, :], ALU.add).then_inc(z2_ready, 1)
                dve.wait_ge(z2_ready, c + 1)
                moments(z2, stats2, mean_var2, var_eps2, ln2_step, c)

            def finish(c):
                dve.wait_ge(y_stored, (c + 1) * DMA)
                normalise(z2, mean_var2, rstd2, y, ln2_rstd, y_ready, c)

            dve.wait_ge(consts_loaded, N_CONST_DMAS * DMA)
            nc.vector.tensor_scalar(w["wvv"][:, :, :], w["wvv"][:, :, :], 0.5, None, ALU.mult).then_inc(consts_ready, 1)
            nc.vector.memset(ones[:, :], 1.0).then_inc(consts_ready, 1)

            def pair(g, ahead, finishes):
                score(g, 0)
                if finishes:
                    take_o(g - LAG)
                score(g, 1)
                if finishes:
                    normalise(z, mean_var, rstd, x1, ln1_rstd, x1_ready, g - LAG)
                weigh(g, 0)
                if finishes:
                    mix(g - LAG)
                weigh(g, 1)
                if finishes:
                    take_vv(g - LAG)
                    finish(g - LAG)

            loops(dve, pair)
            with dve.Fori(SLICES - LAG, SLICES) as c:
                take_o(c)
                normalise(z, mean_var, rstd, x1, ln1_rstd, x1_ready, c)
                mix(c)
                take_vv(c)
                finish(c)

        @block.gpsimd
        def _(pool):
            def carry_in(c):
                nc.gpsimd.tensor_copy(x1_t[:, :, 0:1], carry[:, :, ds(c & 7, 1)]).then_inc(carry_ready, 1)

            def rsqrt(dst, src, step, ready, c):
                pool.wait_ge(step, (c + 1) * 5)
                nc.gpsimd.tensor_tensor(dst[:, :], src[:, :], minus_half[:, :], ALU.pow).then_inc(ready, 1)

            def differ(c):
                pool.wait_ge(xt_taken, c + 1)
                nc.gpsimd.tensor_tensor(diff[:, :, :], x1_t[:, :, 1:1 + SLICE], x1_t[:, :, 0:SLICE], ALU.subtract
                                        ).then_inc(diff_ready, 1)
                nc.gpsimd.tensor_copy(carry[:, :, ds((c & 7) + 1, 1)], x1_t[:, :, SLICE:SLICE + 1])

            def square(c):
                pool.wait_ge(kk_taken, c + 1)
                nc.gpsimd.tensor_tensor(k_act[:, :, :], k_relu[:, :, :], k_relu[:, :, :], ALU.mult).then_inc(kact_ready, 1)

            def score(g, i):
                pool.wait_ge(qk_taken, 4 * g + 2 * (i + 1))
                pool.wait_ge(raw_done, 2 * g + i + 1)
                score_product(nc.gpsimd, i, HEADS - HALF, HEADS).then_inc(sprod_high, 1)

            def weigh(g, i):
                pool.wait_ge(v_taken, 2 * g + i + 1)
                pool.wait_ge(exp_done, 2 * g + i + 1)
                value_product(nc.gpsimd, i, HEADS - HALF, HEADS).then_inc(vprod_high, 1)

            nc.gpsimd.memset(ident[:, :], 0.0).then_inc(ident_zero, 1)
            pool.wait_ge(ident_zero, 1)
            nc.gpsimd.affine_select(out=ident[:, :], in_=ident[:, :], compare_op=ALU.not_equal, fill=1.0, base=0,
                                    pattern=[[-1, P]], channel_multiplier=1)
            nc.gpsimd.memset(minus_half[:, :], -0.5)
            nc.gpsimd.memset(carry[:, :, :], 0.0).then_inc(consts_ready, 1)
            nc.gpsimd.memset(credit[:, 0:1], 0.0).then_inc(z_ready, 1)
            nc.gpsimd.memset(credit[:, 1:2], 0.0).then_inc(y_stored, DMA)
            nc.gpsimd.memset(credit[:, 2:3], 0.0).then_inc(raw_done, 2)
            for i in range(2):
                nc.gpsimd.memset(credit[:, 3 + i:4 + i], 0.0).then_inc(attn_stored[i], DMA)

            def pair(g, ahead, finishes):
                score(g, 0)
                score(g, 1)
                if finishes:
                    carry_in(g - LAG)
                    rsqrt(rstd, var_eps, ln1_step, ln1_rstd, g - LAG)
                weigh(g, 0)
                if finishes:
                    differ(g - LAG)
                weigh(g, 1)
                if finishes:
                    square(g - LAG)
                    rsqrt(rstd2, var_eps2, ln2_step, ln2_rstd, g - LAG)

            loops(pool, pair)
            with pool.Fori(SLICES - LAG, SLICES) as c:
                carry_in(c)
                rsqrt(rstd, var_eps, ln1_step, ln1_rstd, c)
                differ(c)
                square(c)
                rsqrt(rstd2, var_eps2, ln2_step, ln2_rstd, c)


def kernel(L0_attn_x, L0_attn_Wq, L0_attn_bq, L0_attn_Wk, L0_attn_bk, L0_attn_Wv, L0_attn_bv, L0_attn_Wo, L0_attn_bo,
           L0_ffn_W_r, L0_ffn_W_k, L0_ffn_W_v, L0_ffn_mu_r, L0_ffn_mu_k):
    import numpy as np
    import concourse.bacc as bacc
    from concourse.bass_utils import run_bass_kernel_spmd

    x = np.ascontiguousarray(L0_attn_x).reshape(BATCH * SEQ, E)
    laid = {
        "x_tok": x, "x_t": x.T, "wqk_t": np.concatenate([L0_attn_Wq, L0_attn_Wk]).T, "wv_t": L0_attn_Wv.T,
        "wo_t": L0_attn_Wo.T, "wr_t": L0_ffn_W_r.T, "wkk_t": L0_ffn_W_k.T, "wvv_t": L0_ffn_W_v.T,
        "bqk": np.concatenate([L0_attn_bq, L0_attn_bk]), "bv": L0_attn_bv, "bo": L0_attn_bo,
        "mu_r": L0_ffn_mu_r.reshape(ECH, P).T, "mu_k": L0_ffn_mu_k.reshape(ECH, P).T,
    }
    nc = bacc.Bacc("TRN2", target_bir_lowering=False, num_devices=1)
    arrays, args = {}, []
    for name, a in laid.items():
        a = np.ascontiguousarray(a)
        arrays[name] = a
        args.append(nc.dram_tensor(name, a.shape, mybir.dt.from_np(a.dtype), kind="ExternalInput").ap())
    args.append(nc.dram_tensor("y_out", (BATCH * SEQ, E), F32, kind="ExternalOutput").ap())
    build(nc, *args)
    r = run_bass_kernel_spmd(nc, [arrays], core_ids=[0])
    return r.results[0]["y_out"].reshape(BATCH, SEQ, E)
```

```python
from contextlib import ExitStack

import concourse.bass as bass
from concourse import mybir

ALU = mybir.AluOpType
ACT = mybir.ActivationFunctionType
AX = mybir.AxisListType
F32, BF16 = mybir.dt.float32, mybir.dt.bfloat16
ds = bass.ds

P = 128
BATCH, SEQ, E, HEADS = 4, 2048, 256, 16
D = E // HEADS
ECH = E // P
SLICE = 2 * P
SLICES = BATCH * SEQ // SLICE
LAG = SEQ // SLICE
TOK = P // HEADS
GROUPS = SLICE // TOK
OCT = 8
OCTS = GROUPS // OCT
BLOCKS = 6
Q_BLOCKS = ((0, 3), (1, 2), (2, 1))
PARTS_K = BLOCKS * D
ROWS = PARTS_K + TOK
MASK = -1.0e30
SCALE = float(D) ** -0.5
EPS = 1e-5
DMA = 16


def build(nc, x_tok, x_t, wqk_t, wv_t, wo_t, wr_t, wkk_t, wvv_t, b_qk, bv, bo, mu_r, mu_k, out):
    parts_dram = nc.dram_tensor("parts_dram", [SLICES, 2, 3, E, SLICE], BF16).ap()
    v_dram = nc.dram_tensor("v_dram", [SLICES, HEADS, SLICE, D], F32).ap()
    heads_out = nc.dram_tensor("heads_out", [BATCH + 1, HEADS, SEQ, D], F32).ap()

    with ExitStack() as ctx:
        def sb(name, shape, dt=F32):
            return ctx.enter_context(nc.sbuf_tensor(name, shape, dt))

        def ps(name, banks=1):
            return ctx.enter_context(nc.psum_tensor(name, [P, 512 * banks], F32))

        def sem(name):
            return ctx.enter_context(nc.semaphore(name))

        w_dram = {"wqk": wqk_t, "wv": wv_t, "wo": wo_t, "wr": wr_t, "wkk": wkk_t, "wvv": wvv_t}
        w = {n: sb(n + "_sb", [P, ECH, a.shape[1]]) for n, a in w_dram.items()}
        mu = sb("mu", [P, 2, ECH])
        b_col = sb("b_col", [P, 2 * ECH])
        bv_row = sb("bv_row", [P, E])
        bo_row = sb("bo_row", [P, E])
        ident = sb("ident", [P, P])
        ident_h = sb("ident_h", [P, P], BF16)
        select = sb("select", [PARTS_K, GROUPS, P], BF16)
        minus_half = sb("minus_half", [P, 2])
        credit = sb("credit", [P, 9])

        xt = [sb(f"xt{i}", [P, ECH, SLICE]) for i in range(2)]
        full = [sb(f"full{j}", [P, ECH, SLICE]) for j in range(2)]
        rest = [sb(f"rest{j}", [P, ECH, SLICE]) for j in range(2)]
        parts = sb("parts", [P, 2, 3, ECH, SLICE], BF16)
        v_sb = sb("v_sb", [P, 2, E])

        qp = [sb(f"qp{i}", [ROWS, HEADS, SLICE], BF16) for i in range(2)]
        kp = [sb(f"kp{i}", [ROWS, HEADS, SLICE], BF16) for i in range(2)]
        vp = [sb(f"vp{i}", [P, GROUPS, D + 1]) for i in range(2)]
        maxima = sb("maxima", [P, GROUPS])
        max_rest = sb("max_rest", [P, GROUPS])
        max_parts = sb("max_parts", [P, 3, GROUPS], BF16)
        max_t = sb("max_t", [PARTS_K, P], BF16)
        probs = [sb(f"probs{o}", [P, OCT, P]) for o in range(OCTS)]
        inv_sum = sb("inv_sum", [P, GROUPS])
        attn = sb("attn", [P, GROUPS, D])

        yrow = sb("yrow", [P, 2, E])
        attn_t = sb("attn_t", [P, ECH, SLICE])
        xrow = sb("xrow", [P, 2, E])
        xb = sb("xb", [P, 2, E])
        z = sb("z", [P, 2, E])
        stats = sb("stats", [P, 2, 6])
        mean_var = sb("mean_var", [P, 2, 2])
        var_eps = sb("var_eps", [P, 2])
        rstd = sb("rstd", [P, 2])
        x1 = sb("x1", [P, 2, E])
        x1_t = sb("x1_t", [P, ECH, 1 + SLICE])
        carry = sb("carry", [P, ECH, LAG + 1])
        diff = sb("diff", [P, ECH, SLICE])
        xr = sb("xr", [P, ECH, SLICE])
        xk = sb("xk", [P, ECH, SLICE])
        gate_tanh = sb("gate_tanh", [P, 2, E])
        k_relu = sb("k_relu", [P, ECH, SLICE])
        k_act = sb("k_act", [P, ECH, SLICE])
        gated = sb("gated", [P, 2, E])
        z2 = sb("z2", [P, 2, E])
        stats2 = sb("stats2", [P, 2, 6])
        mean_var2 = sb("mean_var2", [P, 2, 2])
        var_eps2 = sb("var_eps2", [P, 2])
        rstd2 = sb("rstd2", [P, 2])
        y = sb("y", [P, 2, E])

        s_ps = [ps(f"s_ps{i}", 2) for i in range(2)]
        pv_ps = ps("pv_ps")
        bank_a, bank_b, bank_c = ps("bank_a"), ps("bank_b"), ps("bank_c")

        consts_loaded, zeroed, scaled, tables = sem("consts_loaded"), sem("zeroed"), sem("scaled"), sem("tables")
        x_loaded = [sem(f"x_loaded{i}") for i in range(2)]
        q_ready, q_taken, k_ready, k_taken = sem("q_ready"), sem("q_taken"), sem("k_ready"), sem("k_taken")
        v_ready, v_taken = sem("v_ready"), sem("v_taken")
        hi_done, rest_done, mid_done, lo_done = sem("hi_done"), sem("rest_done"), sem("mid_done"), sem("lo_done")
        parts_stored, v_stored = sem("parts_stored"), sem("v_stored")
        qk_loaded = [sem(f"qk_loaded{i}") for i in range(2)]
        v_loaded = [sem(f"v_loaded{i}") for i in range(2)]
        rows_ready, max_done, maxp_step = sem("rows_ready"), sem("max_done"), sem("maxp_step")
        mt_ready, mt_taken = sem("mt_ready"), sem("mt_taken")
        cols_ready, exp_done, pv_ready = sem("cols_ready"), sem("exp_done"), sem("pv_ready")
        inv_done, attn_done, attn_stored = sem("inv_done"), sem("attn_done"), [sem(f"attn_stored{h}") for h in range(2)]
        y_loaded, x_rows_loaded, xb_ready = sem("y_loaded"), sem("x_rows_loaded"), sem("xb_ready")
        yt_ready, yt_taken, o_ready, z_ready = sem("yt_ready"), sem("yt_taken"), sem("o_ready"), sem("z_ready")
        ln1_step, ln1_rstd, x1_ready = sem("ln1_step"), sem("ln1_rstd"), sem("x1_ready")
        xt_ready, xt_taken, carry_ready = sem("xt_ready"), sem("xt_taken"), sem("carry_ready")
        diff_ready, mix_ready = sem("diff_ready"), sem("mix_ready")
        r_ready, r_taken, kk_ready, kk_taken = sem("r_ready"), sem("r_taken"), sem("kk_ready"), sem("kk_taken")
        kact_ready, vv_ready, vv_taken, z2_ready = sem("kact_ready"), sem("vv_ready"), sem("vv_taken"), sem("z2_ready")
        ln2_step, ln2_rstd, y_ready, y_stored = sem("ln2_step"), sem("ln2_rstd"), sem("y_ready"), sem("y_stored")

        N_CONST_DMAS = 6 + 2 + 3
        N_LOAD_DMAS = 6
        N_TABLES = 10
        block = ctx.enter_context(nc.Block())

        def loops(engine, body):
            with engine.Fori(0, LAG // 2) as m:
                for i in range(2):
                    body(2 * m + i, i, True, True, False)
            with engine.Fori(LAG // 2, SLICES // 2 - 1) as m:
                for i in range(2):
                    body(2 * m + i, i, True, True, True)
            body(SLICES - 2, 0, False, True, True)
            body(SLICES - 1, 1, False, False, True)

        def flat(t):
            return t[:, :, :].rearrange("p a b -> p (a b)")

        @block.sync
        def _(sp):
            def load_x(a, i):
                sp.dma_start(xt[i][:, :, :], x_t.rearrange("(c p) n -> p c n", p=P)[:, :, ds(a * SLICE, SLICE)]
                             ).then_inc(x_loaded[i], DMA)

            def store_v(a):
                sp.wait_ge(v_taken, a + 1)
                for t in range(2):
                    sp.dma_start(v_dram[a][:, t * P:(t + 1) * P, :].rearrange("h p d -> p h d"),
                                 v_sb[:, t, :].rearrange("p (h d) -> p h d", d=D)).then_inc(v_stored, DMA)

            def store_parts(a):
                sp.wait_ge(lo_done, 2 * a + 2)
                sp.dma_start(parts_dram[a].rearrange("j r (c p) n -> p (j r c) n", p=P),
                             parts[:, :, :, :, :].rearrange("p j r c n -> p (j r c) n")).then_inc(parts_stored, DMA)

            def load_qkv(a, i):
                sp.wait_ge(parts_stored, (a + 2) * DMA)
                row = 0
                for part, n in Q_BLOCKS:
                    q = parts_dram[a, 0, part].rearrange("(o d h) n -> o d (h n)", o=1, d=D).broadcast_to([n, D, HEADS * SLICE])
                    k = parts_dram[a, 1, 0:n].rearrange("r (d h) n -> (r d) (h n)", d=D)
                    for dst, src in ((qp, q), (kp, k)):
                        sp.dma_start(dst[i][row:row + n * D, :, :].rearrange("p h n -> p (h n)"), src).then_inc(qk_loaded[i], DMA)
                    row += n * D
                sp.wait_ge(v_stored, (a + 2) * 2 * DMA)
                sp.dma_start(vp[i][:, :, 0:D], v_dram[a].rearrange("h (t g) d -> (h t) g d", t=TOK)
                             ).then_inc(v_loaded[i], DMA)

            def load_finish(c):
                rows = heads_out[c >> 3].rearrange("h s d -> (h s d)").rearrange("(r f) -> r f", f=E)
                sp.dma_start(yrow[:, :, :], rows[ds((c & 7) * SLICE, SLICE), :].rearrange("(t p) f -> p t f", p=P)
                             ).then_inc(y_loaded, DMA)
                if not (isinstance(c, int) and c == 0):
                    sp.wait_ge(xb_ready, c)
                sp.dma_start(xrow[:, :, :], x_tok[ds(c * SLICE, SLICE), :].rearrange("(t p) f -> p t f", p=P)
                             ).then_inc(x_rows_loaded, DMA)

            def store_y(c):
                sp.wait_ge(y_ready, 2 * (c + 1))
                sp.dma_start(out[ds(c * SLICE, SLICE), :].rearrange("(t p) f -> p t f", p=P), y[:, :, :]
                             ).then_inc(y_stored, DMA)

            load_x(0, 0)
            for n, a in w_dram.items():
                sp.dma_start(w[n][:, :, :], a.rearrange("(c p) f -> p c f", p=P)).then_inc(consts_loaded, DMA)
            for i, a in enumerate((mu_r, mu_k)):
                sp.dma_start(mu[:, i, :], a).then_inc(consts_loaded, DMA)
            sp.dma_start(b_col[:, :], b_qk).then_inc(consts_loaded, DMA)
            for dst, a in ((bv_row, bv), (bo_row, bo)):
                sp.dma_start(dst[:, :], a.rearrange("(o f) -> o f", o=1).broadcast_to([P, E])).then_inc(consts_loaded, DMA)
            load_x(1, 1)
            for a in range(2):
                store_v(a)
                store_parts(a)
                load_qkv(a, a)
                if a == 0:
                    sp.wait_ge(k_ready, 1)
                    load_x(2, 0)

            def body(g, i, ahead, scored, finishes):
                if ahead:
                    store_v(g + 2)
                    load_x((g + 3) & (SLICES - 1), 1 - i)
                for half in range(2):
                    sp.wait_ge(attn_done, 2 * g + half + 2)
                    cols = slice(half * GROUPS // 2, (half + 1) * GROUPS // 2)
                    dst = heads_out[g >> 3, :, ds((g & 7) * SLICE, SLICE), :].rearrange("h (t g) d -> h t g d", t=TOK)
                    sp.dma_start(dst[:, :, cols, :].rearrange("h t g d -> h t (g d)"), attn[:, cols, :]
                                 ).then_inc(attn_stored[half], DMA)
                if finishes:
                    for half in range(2):
                        sp.wait_ge(attn_stored[half], (g + 2) * DMA)
                    load_finish(g - LAG + 1)
                if ahead:
                    store_parts(g + 2)
                    sp.wait_ge(pv_ready, 2 * (g + 2))
                    load_qkv(g + 2, i)
                if finishes:
                    store_y(g - LAG)

            def between():
                for half in range(2):
                    sp.wait_ge(attn_stored[half], (LAG + 1) * DMA)
                load_finish(0)

            with sp.Fori(0, LAG // 2) as m:
                for i in range(2):
                    body(2 * m + i, i, True, True, False)
            between()
            with sp.Fori(LAG // 2, SLICES // 2 - 1) as m:
                for i in range(2):
                    body(2 * m + i, i, True, True, True)
            body(SLICES - 2, 0, False, True, True)
            body(SLICES - 1, 1, False, False, True)
            with sp.Fori(SLICES - LAG, SLICES - 1) as c:
                sp.wait_ge(yt_ready, c + 1)
                load_finish(c + 1)
                store_y(c)
            store_y(SLICES - 1)
            sp.wait_ge(y_stored, DMA * (SLICES + 1))

        @block.tensor
        def _(pe):
            def rows_by(dst, lhs, name, ready):
                for i in range(2):
                    for c in range(ECH):
                        mm = nc.tensor.matmul(dst[:, i * E:(i + 1) * E], lhs[:, c, i * P:(i + 1) * P], w[name][:, c, :],
                                              start=(c == 0), stop=(c == ECH - 1))
                mm.then_inc(ready, 1)

            def columns_by(dst, rhs, name, first, ready):
                for f in range(ECH):
                    for c in range(ECH):
                        mm = nc.tensor.matmul(dst[:, f * SLICE:(f + 1) * SLICE],
                                              w[name][:, c, first + f * P:first + (f + 1) * P], rhs[:, c, 0:SLICE],
                                              start=(c == 0), stop=(c == ECH - 1))
                mm.then_inc(ready, 1)

            def to_columns(dst, src, ready):
                for ch in range(ECH):
                    for t in range(2):
                        mm = nc.tensor.transpose(dst[:, ch * SLICE + t * P:ch * SLICE + (t + 1) * P],
                                                 src[:, t, ch * P:(ch + 1) * P], ident[:, :])
                mm.then_inc(ready, 1)

            def group_of(t, i, gr):
                return t[i][:, :, :].rearrange("p h (t g) -> p (h t) g", g=GROUPS)[:, :, gr]

            def score_rows(i, o):
                for j in range(OCT):
                    gr = o * OCT + j
                    mm = nc.tensor.matmul(s_ps[o % 2][:, j * P:(j + 1) * P], group_of(qp, i, gr), group_of(kp, i, gr),
                                          start=True, stop=True)
                mm.then_inc(rows_ready, 1)

            def score_columns(i, o):
                for j in range(OCT):
                    gr = o * OCT + j
                    dst = s_ps[o % 2][:, j * P:(j + 1) * P]
                    nc.tensor.matmul(dst, group_of(kp, i, gr), group_of(qp, i, gr), start=True, stop=False)
                    mm = nc.tensor.matmul(dst, select[:, gr, :], max_t[:, :], start=False, stop=True)
                mm.then_inc(cols_ready, 1)

            def weigh(i, o):
                for j in range(OCT):
                    at = (o % 2) * OCT + j
                    mm = nc.tensor.matmul(pv_ps[:, at * (D + 1):(at + 1) * (D + 1)], probs[o][:, j, :],
                                          vp[i][:, o * OCT + j, :], start=True, stop=True)
                if o % 2:
                    mm.then_inc(pv_ready, 1)

            def turn_maxima(ready):
                mm = nc.tensor.matmul(bank_b[0:PARTS_K, 0:P], max_parts[:, :, :].rearrange("p r g -> p (r g)"),
                                      ident_h[:, :], start=True, stop=True)
                mm.then_inc(ready, 1)

            def score_all_rows(a, i, which):
                for o in which:
                    if o >= 2:
                        pe.wait_ge(max_done, OCTS * a + o - 1)
                    score_rows(i, o)

            pe.wait_ge(consts_loaded, N_CONST_DMAS * DMA)
            pe.wait_ge(scaled, 3)
            for a in range(2):
                pe.wait_ge(x_loaded[a], DMA)
                if a:
                    pe.wait_ge(v_taken, 1)
                rows_by(bank_c, xt[a], "wv", v_ready)
                if a:
                    pe.wait_ge(q_taken, 2)
                columns_by(bank_a, xt[a], "wqk", 0, q_ready)
                if a:
                    pe.wait_ge(k_taken, 2)
                columns_by(bank_b, xt[a], "wqk", E, k_ready)
            pe.wait_ge(tables, N_TABLES)
            pe.wait_ge(qk_loaded[0], N_LOAD_DMAS * DMA)
            score_all_rows(0, 0, range(OCTS))
            pe.wait_ge(maxp_step, 4)
            pe.wait_ge(k_taken, 4)
            turn_maxima(mt_ready)

            def body(g, i, ahead, scored, finishes):
                c = g - LAG
                if finishes:
                    pe.wait_ge(y_loaded, (c + 1) * DMA)
                    pe.wait_ge(kk_taken, c + 1)
                    pe.wait_ge(q_taken, 2 * (g + 2) if ahead else 2 * SLICES)
                    to_columns(bank_a, yrow, yt_ready)
                if ahead:
                    pe.wait_ge(x_loaded[i], x_count(g, i))
                    pe.wait_ge(v_taken, g + 2)
                    if finishes:
                        pe.wait_ge(vv_taken, c + 1)
                    rows_by(bank_c, xt[i], "wv", v_ready)
                pe.wait_ge(mt_taken, g + 1)
                for o in range(2):
                    pe.wait_ge(max_done, OCTS * g + o + 3)
                    score_columns(i, o)
                if finishes:
                    pe.wait_ge(yt_taken, c + 1)
                    rows_by(bank_b, attn_t, "wo", o_ready)
                pe.wait_ge(exp_done, OCTS * g + 1)
                score_columns(i, 2)
                pe.wait_ge(v_loaded[i], v_count(g, i))
                pe.wait_ge(attn_done, 2 * g + 1)
                weigh(i, 0)
                pe.wait_ge(exp_done, OCTS * g + 2)
                score_columns(i, 3)
                weigh(i, 1)
                if ahead:
                    pe.wait_ge(q_taken, 2 * (g + 2))
                    if finishes:
                        pe.wait_ge(yt_taken, c + 1)
                    columns_by(bank_a, xt[i], "wqk", 0, q_ready)
                    if finishes:
                        pe.wait_ge(z_ready, c + 2)
                    columns_by(bank_b, xt[i], "wqk", E, k_ready)
                pe.wait_ge(attn_done, 2 * g + 2)
                pe.wait_ge(exp_done, OCTS * g + 3)
                weigh(i, 2)
                pe.wait_ge(exp_done, OCTS * g + 4)
                weigh(i, 3)
                if finishes:
                    pe.wait_ge(x1_ready, 2 * (c + 1))
                    if ahead:
                        pe.wait_ge(q_taken, 2 * (g + 3))
                    to_columns(bank_a, x1, xt_ready)
                if scored:
                    pe.wait_ge(qk_loaded[1 - i], qk_count(g, i))
                    score_all_rows(g + 1, 1 - i, range(0, 2))
                if finishes:
                    pe.wait_ge(mix_ready, 4 * c + 4)
                    if ahead:
                        pe.wait_ge(k_taken, 2 * (g + 3))
                    rows_by(bank_b, xr, "wr", r_ready)
                    columns_by(bank_a, xk, "wkk", 0, kk_ready)
                if scored:
                    score_all_rows(g + 1, 1 - i, range(2, OCTS))
                    pe.wait_ge(maxp_step, 4 * (g + 2))
                    if finishes:
                        pe.wait_ge(r_taken, c + 1)
                    else:
                        pe.wait_ge(k_taken, 2 * (g + 3))
                    turn_maxima(mt_ready)
                if finishes:
                    pe.wait_ge(kact_ready, c + 1)
                    if ahead:
                        pe.wait_ge(v_taken, g + 3)
                    else:
                        pe.wait_ge(vv_taken, c + 1)
                    rows_by(bank_c, k_act, "wvv", vv_ready)

            def x_count(g, i):
                return ((g >> 1) + 2) * DMA

            def v_count(g, i):
                return ((g >> 1) + 1) * DMA

            def qk_count(g, i):
                return ((g + 1 >> 1) + 1) * DMA * N_LOAD_DMAS

            loops(pe, body)
            with pe.Fori(SLICES - LAG, SLICES) as c:
                pe.wait_ge(y_loaded, (c + 1) * DMA)
                pe.wait_ge(kk_taken, c + 1)
                to_columns(bank_a, yrow, yt_ready)
                pe.wait_ge(r_taken, c)
                pe.wait_ge(yt_taken, c + 1)
                rows_by(bank_b, attn_t, "wo", o_ready)
                pe.wait_ge(x1_ready, 2 * (c + 1))
                to_columns(bank_a, x1, xt_ready)
                pe.wait_ge(mix_ready, 4 * c + 4)
                columns_by(bank_a, xk, "wkk", 0, kk_ready)
                rows_by(bank_b, xr, "wr", r_ready)
                pe.wait_ge(kact_ready, c + 1)
                pe.wait_ge(vv_taken, c + 1)
                rows_by(bank_c, k_act, "wvv", vv_ready)

        @block.scalar
        def _(act):
            def take_projection(a, j, src, ready, taken):
                act.wait_ge(ready, a + 1)
                act.wait_ge(rest_done, 2 * a + j + 1)
                for ch in range(ECH):
                    nc.scalar.activation(full[j][:, ch, :], src[:, ch * SLICE:(ch + 1) * SLICE], ACT.Identity,
                                         bias=b_col[:, j * ECH + ch:j * ECH + ch + 1]).then_inc(taken, 1)
                act.wait_ge(parts_stored, (a + 1) * DMA)
                act.wait_ge(taken, 2 * (a + 1))
                nc.scalar.activation(parts[:, j, 0, :, :], full[j][:, :, :], ACT.Copy).then_inc(hi_done, 1)

            def middle(a, j):
                act.wait_ge(rest_done, 2 * a + j + 3)
                nc.scalar.activation(parts[:, j, 1, :, :], rest[j][:, :, :], ACT.Copy).then_inc(mid_done, 1)

            def take_maxima(a):
                act.wait_ge(mt_ready, a + 1)
                nc.scalar.activation(max_t[:, :], bank_b[0:PARTS_K, 0:P], ACT.Copy).then_inc(mt_taken, 1)

            def take_yt(c):
                act.wait_ge(yt_ready, c + 1)
                nc.scalar.activation(flat(attn_t), bank_a[:, :], ACT.Copy).then_inc(yt_taken, 1)

            def take_x1_t(c):
                act.wait_ge(xt_ready, c + 1)
                act.wait_ge(carry_ready, c + 1)
                nc.scalar.activation(x1_t[:, :, 1:1 + SLICE], bank_a[:, :].rearrange("p (c n) -> p c n", c=ECH), ACT.Copy
                                     ).then_inc(xt_taken, 1)

            def take_r(c):
                act.wait_ge(r_ready, c + 1)
                nc.scalar.activation(flat(gate_tanh), bank_b[:, :], ACT.Tanh, scale=0.5).then_inc(r_taken, 1)

            def take_kk(c):
                act.wait_ge(kk_ready, c + 1)
                nc.scalar.activation(flat(k_relu), bank_a[:, :], ACT.Relu).then_inc(kk_taken, 1)

            act.wait_ge(scaled, 3)
            for a in range(2):
                take_projection(a, 0, bank_a, q_ready, q_taken)
                take_projection(a, 1, bank_b, k_ready, k_taken)
                middle(a, 0)
                middle(a, 1)
            take_maxima(0)

            def body(g, i, ahead, scored, finishes):
                c = g - LAG
                if finishes:
                    take_yt(c)
                for o in range(OCTS):
                    act.wait_ge(cols_ready, OCTS * g + o + 1)
                    if o % 2 == 0:
                        act.wait_ge(pv_ready, 2 * g + o // 2 + 1)
                    nc.scalar.activation(flat(probs[o]), s_ps[o % 2][:, :], ACT.Exp).then_inc(exp_done, 1)
                if ahead:
                    take_projection(g + 2, 0, bank_a, q_ready, q_taken)
                    take_projection(g + 2, 1, bank_b, k_ready, k_taken)
                if finishes:
                    take_x1_t(c)
                if ahead:
                    middle(g + 2, 0)
                    middle(g + 2, 1)
                if finishes:
                    take_r(c)
                    take_kk(c)
                if scored:
                    take_maxima(g + 1)

            loops(act, body)
            with act.Fori(SLICES - LAG, SLICES) as c:
                take_yt(c)
                take_x1_t(c)
                take_kk(c)
                take_r(c)

        @block.vector
        def _(dve):
            def take_v(a):
                dve.wait_ge(v_ready, a + 1)
                dve.wait_ge(v_stored, (a + 1) * 2 * DMA)
                bias = bv_row[:, :].rearrange("p (o f) -> p o f", o=1).broadcast_to([P, 2, E])
                nc.vector.tensor_tensor(v_sb[:, :, :], bank_c[:, :].rearrange("p (t f) -> p t f", t=2), bias, ALU.add
                                        ).then_inc(v_taken, 1)

            def rests(a, j):
                dve.wait_ge(hi_done, 2 * a + j + 1)
                nc.vector.tensor_tensor(rest[j][:, :, :], full[j][:, :, :], parts[:, j, 0, :, :], ALU.subtract
                                        ).then_inc(rest_done, 1)

            def lows(a, j):
                dve.wait_ge(mid_done, 2 * a + j + 1)
                nc.vector.tensor_tensor(parts[:, j, 2, :, :], rest[j][:, :, :], parts[:, j, 1, :, :], ALU.subtract
                                        ).then_inc(lo_done, 1)

            def maxes(a, which):
                for o in which:
                    dve.wait_ge(rows_ready, OCTS * a + o + 1)
                    nc.vector.tensor_reduce(maxima[:, o * OCT:(o + 1) * OCT],
                                            s_ps[o % 2][:, :].rearrange("p (g n) -> p g n", g=OCT), AX.X, ALU.max
                                            ).then_inc(max_done, 1)

            def max_split(a):
                dve.wait_ge(max_done, OCTS * (a + 1))
                nc.vector.tensor_copy(max_parts[:, 0, :], maxima[:, :]).then_inc(maxp_step, 1)
                dve.wait_ge(maxp_step, 4 * a + 1)
                nc.vector.tensor_tensor(max_rest[:, :], maxima[:, :], max_parts[:, 0, :], ALU.subtract).then_inc(maxp_step, 1)
                dve.wait_ge(maxp_step, 4 * a + 2)
                nc.vector.tensor_copy(max_parts[:, 1, :], max_rest[:, :]).then_inc(maxp_step, 1)
                dve.wait_ge(maxp_step, 4 * a + 3)
                nc.vector.tensor_tensor(max_parts[:, 2, :], max_rest[:, :], max_parts[:, 1, :], ALU.subtract
                                        ).then_inc(maxp_step, 1)

            def take_attention(g, half):
                cols = slice(half * GROUPS // 2, (half + 1) * GROUPS // 2)
                pv = pv_ps[:, 0:GROUPS // 2 * (D + 1)].rearrange("p (g e) -> p g e", e=D + 1)
                dve.wait_ge(pv_ready, 2 * g + half + 3)
                nc.vector.reciprocal(inv_sum[:, cols], pv[:, :, D]).then_inc(inv_done, 1)
                dve.wait_ge(attn_stored[half], (g + 1) * DMA)
                dve.wait_ge(inv_done, 2 * g + half + 1)
                inv = inv_sum[:, cols].rearrange("p (g o) -> p g o", o=1).broadcast_to([P, GROUPS // 2, D])
                nc.vector.tensor_tensor(attn[:, cols, :], pv[:, :, 0:D], inv, ALU.mult).then_inc(attn_done, 1)

            def moments(src, stats_t, mv, ve, step, c):
                for t in range(2):
                    nc.vector.bn_stats(stats_t[:, t, :], src[:, t, :]).then_inc(step, 1)
                dve.wait_ge(step, c * 5 + 2)
                nc.vector.memset(ve[:, :], 0.0)
                for t in range(2):
                    nc.vector.bn_aggr(mv[:, t, :], stats_t[:, t, :]).then_inc(step, 1)
                dve.wait_ge(step, c * 5 + 4)
                nc.vector.tensor_scalar(ve[:, :], mv[:, :, 1], EPS, None, ALU.add).then_inc(step, 1)

            def take_o(c):
                dve.wait_ge(xb_ready, c + 1)
                dve.wait_ge(o_ready, c + 1)
                nc.vector.tensor_tensor(flat(z), bank_b[:, :], flat(xb), ALU.add).then_inc(z_ready, 1)
                dve.wait_ge(z_ready, c + 2)
                moments(z, stats, mean_var, var_eps, ln1_step, c)

            def normalise(src, mv, rs, dst, rstd_ready, ready, c):
                dve.wait_ge(rstd_ready, c + 1)
                for t in range(2):
                    nc.vector.tensor_scalar(dst[:, t, :], src[:, t, :], mv[:, t, 0:1], rs[:, t:t + 1],
                                            ALU.subtract, ALU.mult).then_inc(ready, 1)

            def mix(c):
                dve.wait_ge(diff_ready, c + 1)
                for i, dst in enumerate((xr, xk)):
                    for ch in range(ECH):
                        nc.vector.scalar_tensor_tensor(out=dst[:, ch, :], in0=diff[:, ch, :], scalar=mu[:, i, ch:ch + 1],
                                                       in1=x1_t[:, ch, 0:SLICE], op0=ALU.mult, op1=ALU.add
                                                       ).then_inc(mix_ready, 1)

            def take_vv(c):
                dve.wait_ge(vv_ready, c + 1)
                dve.wait_ge(r_taken, c + 1)
                nc.vector.scalar_tensor_tensor(out=flat(gated), in0=flat(gate_tanh), scalar=1.0, in1=bank_c[:, :],
                                               op0=ALU.add, op1=ALU.mult).then_inc(vv_taken, 1)
                dve.wait_ge(vv_taken, c + 2)
                nc.vector.tensor_tensor(z2[:, :, :], gated[:, :, :], x1[:, :, :], ALU.add).then_inc(z2_ready, 1)
                dve.wait_ge(z2_ready, c + 1)
                moments(z2, stats2, mean_var2, var_eps2, ln2_step, c)

            def result(c):
                dve.wait_ge(y_stored, (c + 1) * DMA)
                normalise(z2, mean_var2, rstd2, y, ln2_rstd, y_ready, c)

            for t in (ident, ident_h):
                nc.vector.memset(t[:, :], 0.0).then_inc(zeroed, 1)
            nc.vector.memset(select[:, :, :], 0.0).then_inc(zeroed, 1)
            for i in range(2):
                nc.vector.memset(qp[i][PARTS_K:ROWS, :, :], MASK).then_inc(zeroed, 1)
                nc.vector.memset(kp[i][PARTS_K:ROWS, :, :], 0.0).then_inc(zeroed, 1)
                nc.vector.memset(vp[i][:, :, D:D + 1], 1.0).then_inc(zeroed, 1)
            dve.wait_ge(consts_loaded, N_CONST_DMAS * DMA)
            nc.vector.tensor_scalar(w["wvv"][:, :, :], w["wvv"][:, :, :], 0.5, None, ALU.mult).then_inc(scaled, 1)
            nc.vector.tensor_scalar(w["wqk"][:, :, 0:E], w["wqk"][:, :, 0:E], SCALE, None, ALU.mult).then_inc(scaled, 1)
            nc.vector.tensor_scalar(b_col[:, 0:ECH], b_col[:, 0:ECH], SCALE, None, ALU.mult).then_inc(scaled, 1)
            for a in range(2):
                take_v(a)
                for j in range(2):
                    rests(a, j)
                for j in range(2):
                    lows(a, j)
            maxes(0, range(OCTS))
            max_split(0)

            def body(g, i, ahead, scored, finishes):
                c = g - LAG
                if ahead:
                    take_v(g + 2)
                if finishes:
                    take_o(c)
                take_attention(g, 0)
                if finishes:
                    normalise(z, mean_var, rstd, x1, ln1_rstd, x1_ready, c)
                if ahead:
                    rests(g + 2, 0)
                    rests(g + 2, 1)
                take_attention(g, 1)
                if scored:
                    maxes(g + 1, range(0, 2))
                if finishes:
                    mix(c)
                if ahead:
                    lows(g + 2, 0)
                    lows(g + 2, 1)
                if scored:
                    maxes(g + 1, range(2, OCTS))
                    max_split(g + 1)
                if finishes:
                    take_vv(c)
                    result(c)

            loops(dve, body)
            with dve.Fori(SLICES - LAG, SLICES) as c:
                take_o(c)
                normalise(z, mean_var, rstd, x1, ln1_rstd, x1_ready, c)
                mix(c)
                take_vv(c)
                result(c)

        @block.gpsimd
        def _(pool):
            def add_bias(c):
                pool.wait_ge(x_rows_loaded, (c + 1) * DMA)
                pool.wait_ge(z_ready, c + 1)
                bias = bo_row[:, :].rearrange("p (o f) -> p o f", o=1).broadcast_to([P, 2, E])
                nc.gpsimd.tensor_tensor(xb[:, :, :], xrow[:, :, :], bias, ALU.add).then_inc(xb_ready, 1)

            def carry_in(c):
                nc.gpsimd.tensor_copy(x1_t[:, :, 0:1], carry[:, :, ds(c & 7, 1)]).then_inc(carry_ready, 1)

            def rsqrt(dst, src, step, ready, c):
                pool.wait_ge(step, (c + 1) * 5)
                nc.gpsimd.tensor_tensor(dst[:, :], src[:, :], minus_half[:, :], ALU.pow).then_inc(ready, 1)

            def differ(c):
                pool.wait_ge(xt_taken, c + 1)
                nc.gpsimd.tensor_tensor(diff[:, :, :], x1_t[:, :, 1:1 + SLICE], x1_t[:, :, 0:SLICE], ALU.subtract
                                        ).then_inc(diff_ready, 1)
                nc.gpsimd.tensor_copy(carry[:, :, ds((c & 7) + 1, 1)], x1_t[:, :, SLICE:SLICE + 1])

            def square(c):
                pool.wait_ge(kk_taken, c + 2)
                nc.gpsimd.tensor_tensor(k_act[:, :, :], k_relu[:, :, :], k_relu[:, :, :], ALU.mult).then_inc(kact_ready, 1)

            for n, (s, by) in enumerate(((z_ready, 1), (y_stored, DMA), (attn_done, 1), (attn_stored[0], DMA), (attn_stored[1], DMA),
                                         (rest_done, 2), (vv_taken, 1), (kk_taken, 1), (pv_ready, 2))):
                nc.gpsimd.memset(credit[:, n:n + 1], 0.0).then_inc(s, by)
            nc.gpsimd.memset(minus_half[:, 0:1], -0.5).then_inc(parts_stored, DMA)
            nc.gpsimd.memset(minus_half[:, 1:2], -0.5).then_inc(v_stored, 2 * DMA)

            nc.gpsimd.memset(carry[:, :, :], 0.0).then_inc(tables, 1)
            pool.wait_ge(zeroed, 9)
            tables_done = 1
            for t in (ident, ident_h):
                pool.wait_ge(tables, tables_done)
                nc.gpsimd.affine_select(out=t[:, :], in_=t[:, :], compare_op=ALU.not_equal, fill=1.0, base=0,
                                        pattern=[[-1, P]], channel_multiplier=1).then_inc(tables, 1)
                tables_done += 1
            for r in range(3):
                rows = select[r * GROUPS:(r + 1) * GROUPS, :, :]
                pool.wait_ge(tables, tables_done)
                nc.gpsimd.affine_select(out=rows, in_=rows, compare_op=ALU.not_equal, fill=-1.0, base=0,
                                        pattern=[[-1, GROUPS], [0, P]], channel_multiplier=1).then_inc(tables, 1)
                tables_done += 1
            for i in range(2):
                for t, fill in ((qp, 0.0), (kp, 1.0)):
                    rows = t[i][PARTS_K:ROWS, :, :].rearrange("r h (t g) -> r h t g", t=TOK)
                    pool.wait_ge(tables, tables_done)
                    nc.gpsimd.affine_select(out=rows, in_=rows, compare_op=ALU.not_equal, fill=fill, base=0,
                                            pattern=[[0, HEADS], [-1, TOK], [0, GROUPS]], channel_multiplier=1
                                            ).then_inc(tables, 1)
                    tables_done += 1
            pool.wait_ge(tables, tables_done)

            with pool.Fori(0, SLICES) as c:
                add_bias(c)
                carry_in(c)
                rsqrt(rstd, var_eps, ln1_step, ln1_rstd, c)
                differ(c)
                square(c)
                rsqrt(rstd2, var_eps2, ln2_step, ln2_rstd, c)


def kernel(L0_attn_x, L0_attn_Wq, L0_attn_bq, L0_attn_Wk, L0_attn_bk, L0_attn_Wv, L0_attn_bv, L0_attn_Wo, L0_attn_bo,
           L0_ffn_W_r, L0_ffn_W_k, L0_ffn_W_v, L0_ffn_mu_r, L0_ffn_mu_k):
    import numpy as np
    import concourse.bacc as bacc
    from concourse.bass_utils import run_bass_kernel_spmd

    def by_width(a):
        return a.reshape(HEADS, D, -1).swapaxes(0, 1).reshape(a.shape)

    x = np.ascontiguousarray(L0_attn_x).reshape(BATCH * SEQ, E)
    laid = {
        "x_tok": x, "x_t": x.T, "wqk_t": np.concatenate([by_width(L0_attn_Wq), by_width(L0_attn_Wk)]).T, "wv_t": L0_attn_Wv.T,
        "wo_t": L0_attn_Wo.T, "wr_t": L0_ffn_W_r.T, "wkk_t": L0_ffn_W_k.T, "wvv_t": L0_ffn_W_v.T,
        "b_qk": np.concatenate([by_width(L0_attn_bq).reshape(ECH, P), by_width(L0_attn_bk).reshape(ECH, P)]).T, "bv": L0_attn_bv, "bo": L0_attn_bo,
        "mu_r": L0_ffn_mu_r.reshape(ECH, P).T, "mu_k": L0_ffn_mu_k.reshape(ECH, P).T,
    }
    nc = bacc.Bacc("TRN2", target_bir_lowering=False, num_devices=1)
    arrays, args = {}, []
    for name, a in laid.items():
        a = np.ascontiguousarray(a)
        arrays[name] = a
        args.append(nc.dram_tensor(name, a.shape, mybir.dt.from_np(a.dtype), kind="ExternalInput").ap())
    args.append(nc.dram_tensor("y_out", (BATCH * SEQ, E), F32, kind="ExternalOutput").ap())
    build(nc, *args)
    r = run_bass_kernel_spmd(nc, [arrays], core_ids=[0])
    return r.results[0]["y_out"].reshape(BATCH, SEQ, E)
```

```python
from contextlib import ExitStack

import concourse.bass as bass
from concourse import mybir

ALU = mybir.AluOpType
ACT = mybir.ActivationFunctionType
AX = mybir.AxisListType
F32, BF16 = mybir.dt.float32, mybir.dt.bfloat16
ds = bass.ds

P = 128
BATCH, SEQ, E, HEADS = 4, 2048, 256, 16
D = E // HEADS
ECH = E // P
SLICE = 2 * P
SLICES = BATCH * SEQ // SLICE
LAG = SEQ // SLICE
TOK = P // HEADS
GROUPS = SLICE // TOK
OCT = 8
OCTS = GROUPS // OCT
BLOCKS = 6
Q_BLOCKS = ((0, 3), (1, 2), (2, 1))
PARTS_K = BLOCKS * D
ROWS = PARTS_K + TOK
MASK = -1.0e30
SCALE = float(D) ** -0.5
EPS = 1e-5
DMA = 16


def build(nc, x_tok, x_t, wqk_t, wv_t, wo_t, wr_t, wkk_t, wvv_t, b_qk, bv, bo, mu_r, mu_k, out):
    parts_dram = nc.dram_tensor("parts_dram", [SLICES, 2, 3, E, SLICE], BF16).ap()
    v_dram = nc.dram_tensor("v_dram", [SLICES, HEADS, SLICE, D], F32).ap()
    heads_out = nc.dram_tensor("heads_out", [BATCH + 1, HEADS, SEQ, D], F32).ap()

    with ExitStack() as ctx:
        def sb(name, shape, dt=F32):
            return ctx.enter_context(nc.sbuf_tensor(name, shape, dt))

        def ps(name, banks=1):
            return ctx.enter_context(nc.psum_tensor(name, [P, 512 * banks], F32))

        def sem(name):
            return ctx.enter_context(nc.semaphore(name))

        w_dram = {"wqk": wqk_t, "wv": wv_t, "wo": wo_t, "wr": wr_t, "wkk": wkk_t, "wvv": wvv_t}
        w = {n: sb(n + "_sb", [P, ECH, a.shape[1]]) for n, a in w_dram.items()}
        mu = sb("mu", [P, 2, ECH])
        b_col = sb("b_col", [P, 2 * ECH])
        bv_row = sb("bv_row", [P, E])
        bo_row = sb("bo_row", [P, E])
        ident = sb("ident", [P, P])
        ident_h = sb("ident_h", [P, P], BF16)
        select = sb("select", [PARTS_K, GROUPS, P], BF16)
        minus_half = sb("minus_half", [P, 2])
        credit = sb("credit", [P, 9])

        xt = [sb(f"xt{i}", [P, ECH, SLICE]) for i in range(2)]
        full = [sb(f"full{j}", [P, ECH, SLICE]) for j in range(2)]
        rest = [sb(f"rest{j}", [P, ECH, SLICE]) for j in range(2)]
        parts = sb("parts", [P, 2, 3, ECH, SLICE], BF16)
        v_sb = sb("v_sb", [P, 2, E])

        qp = [sb(f"qp{i}", [ROWS, HEADS, SLICE], BF16) for i in range(2)]
        kp = [sb(f"kp{i}", [ROWS, HEADS, SLICE], BF16) for i in range(2)]
        vp = [sb(f"vp{i}", [P, GROUPS, 2 * D]) for i in range(2)]
        maxima = sb("maxima", [P, GROUPS])
        max_rest = sb("max_rest", [P, GROUPS])
        max_parts = sb("max_parts", [P, 3, GROUPS], BF16)
        max_t = sb("max_t", [PARTS_K, P], BF16)
        probs = [sb(f"probs{o}", [P, OCT, P]) for o in range(OCTS)]
        weighed_t = sb("weighed_t", [P, 2, P])
        inv_sum = sb("inv_sum", [P, GROUPS])
        attn = sb("attn", [P, GROUPS, D])

        yrow = sb("yrow", [P, 2, E])
        attn_t = sb("attn_t", [P, ECH, SLICE])
        xrow = sb("xrow", [P, 2, E])
        xb = sb("xb", [P, 2, E])
        z = sb("z", [P, 2, E])
        stats = sb("stats", [P, 2, 6])
        mean_var = sb("mean_var", [P, 2, 2])
        var_eps = sb("var_eps", [P, 2])
        rstd = sb("rstd", [P, 2])
        x1 = [sb(f"x1_{i}", [P, 2, E]) for i in range(2)]
        x1_t = sb("x1_t", [P, ECH, 1 + SLICE])
        carry = sb("carry", [P, ECH, LAG + 1])
        diff = sb("diff", [P, ECH, SLICE])
        xr = sb("xr", [P, ECH, SLICE])
        xk = sb("xk", [P, ECH, SLICE])
        gate_tanh = sb("gate_tanh", [P, 2, E])
        k_relu = sb("k_relu", [P, ECH, SLICE])
        k_act = sb("k_act", [P, ECH, SLICE])
        gated = sb("gated", [P, 2, E])
        z2 = sb("z2", [P, 2, E])
        stats2 = sb("stats2", [P, 2, 6])
        mean_var2 = sb("mean_var2", [P, 2, 2])
        var_eps2 = sb("var_eps2", [P, 2])
        rstd2 = sb("rstd2", [P, 2])
        y = sb("y", [P, 2, E])

        s_ps = [ps(f"s_ps{i}", 2) for i in range(2)]
        pv_ps = ps("pv_ps")
        bank_a, bank_b, bank_c = ps("bank_a"), ps("bank_b"), ps("bank_c")

        consts_loaded, zeroed, scaled, tables = sem("consts_loaded"), sem("zeroed"), sem("scaled"), sem("tables")
        identities = sem("identities")
        x_loaded = [sem(f"x_loaded{i}") for i in range(2)]
        q_ready, q_taken, k_ready, k_taken = sem("q_ready"), sem("q_taken"), sem("k_ready"), sem("k_taken")
        v_ready, v_taken = sem("v_ready"), sem("v_taken")
        hi_done, rest_done, mid_done, lo_done = sem("hi_done"), sem("rest_done"), sem("mid_done"), sem("lo_done")
        parts_stored, v_stored = sem("parts_stored"), sem("v_stored")
        qk_loaded = [sem(f"qk_loaded{i}") for i in range(2)]
        v_loaded = [sem(f"v_loaded{i}") for i in range(2)]
        rows_ready, max_done, maxp_step = sem("rows_ready"), sem("max_done"), sem("maxp_step")
        mt_ready, mt_taken = sem("mt_ready"), sem("mt_taken")
        cols_ready, exp_done, pv_ready = sem("cols_ready"), sem("exp_done"), sem("pv_ready")
        weighed, weighed_taken = sem("weighed"), sem("weighed_taken")
        inv_done, attn_done, attn_stored = sem("inv_done"), sem("attn_done"), [sem(f"attn_stored{h}") for h in range(2)]
        y_loaded, x_rows_loaded, xb_ready = sem("y_loaded"), sem("x_rows_loaded"), sem("xb_ready")
        yt_ready, yt_taken, o_ready, z_ready = sem("yt_ready"), sem("yt_taken"), sem("o_ready"), sem("z_ready")
        ln1_step, ln1_rstd, x1_ready = sem("ln1_step"), sem("ln1_rstd"), sem("x1_ready")
        xt_ready, xt_taken = sem("xt_ready"), sem("xt_taken")
        carry_ready, carry_saved = sem("carry_ready"), sem("carry_saved")
        diff_ready, mix_ready = sem("diff_ready"), sem("mix_ready")
        r_ready, r_taken, kk_ready, kk_taken = sem("r_ready"), sem("r_taken"), sem("kk_ready"), sem("kk_taken")
        kact_ready, vv_ready, vv_taken, z2_ready = sem("kact_ready"), sem("vv_ready"), sem("vv_taken"), sem("z2_ready")
        ln2_step, ln2_rstd, y_ready, y_stored = sem("ln2_step"), sem("ln2_rstd"), sem("y_ready"), sem("y_stored")

        N_CONST_DMAS = 6 + 2 + 3
        N_LOAD_DMAS = 3 + BLOCKS
        N_TABLES = 4 + 3 + 2
        block = ctx.enter_context(nc.Block())

        def loops(engine, body):
            with engine.Fori(0, LAG // 2) as m:
                for i in range(2):
                    body(2 * m + i, i, True, True, False, False)
            body(LAG, 0, True, True, True, False)
            body(LAG + 1, 1, True, True, True, True)
            with engine.Fori(LAG // 2 + 1, SLICES // 2 - 1) as m:
                for i in range(2):
                    body(2 * m + i, i, True, True, True, True)
            body(SLICES - 2, 0, False, True, True, True)
            body(SLICES - 1, 1, False, False, True, True)

        def last_slices(engine, body):
            with engine.Fori((SLICES - LAG) // 2, SLICES // 2) as m:
                for i in range(2):
                    body(2 * m + i, i)

        def flat(t):
            return t[:, :, :].rearrange("p a b -> p (a b)")

        @block.sync
        def _(sp):
            def load_x(a, i):
                sp.dma_start(xt[i][:, :, :], x_t.rearrange("(c p) n -> p c n", p=P)[:, :, ds(a * SLICE, SLICE)]
                             ).then_inc(x_loaded[i], DMA)

            def store_v(a):
                sp.wait_ge(v_taken, a + 1)
                for t in range(2):
                    sp.dma_start(v_dram[a][:, t * P:(t + 1) * P, :].rearrange("h p d -> p h d"),
                                 v_sb[:, t, :].rearrange("p (h d) -> p h d", d=D)).then_inc(v_stored, DMA)

            def store_parts(a):
                sp.wait_ge(lo_done, 2 * a + 2)
                sp.dma_start(parts_dram[a].rearrange("j r (c p) n -> p (j r c) n", p=P),
                             parts[:, :, :, :, :].rearrange("p j r c n -> p (j r c) n")).then_inc(parts_stored, DMA)

            def load_qkv(a, i):
                sp.wait_ge(parts_stored, (a + 2) * DMA)
                row = 0
                for part, n in Q_BLOCKS:
                    sp.dma_start(kp[i][row:row + n * D, :, :].rearrange("p h n -> p (h n)"),
                                 parts_dram[a, 1, 0:n].rearrange("r (d h) n -> (r d) (h n)", d=D)).then_inc(qk_loaded[i], DMA)
                    for _ in range(n):
                        sp.dma_start(qp[i][row:row + D, :, :].rearrange("p h n -> p (h n)"),
                                     parts_dram[a, 0, part].rearrange("(d h) n -> d (h n)", d=D)).then_inc(qk_loaded[i], DMA)
                        row += D
                sp.wait_ge(v_stored, (a + 2) * 2 * DMA)
                sp.dma_start(vp[i][:, :, 0:D], v_dram[a].rearrange("h (t g) d -> (h t) g d", t=TOK)
                             ).then_inc(v_loaded[i], DMA)

            def load_finish(c):
                rows = heads_out[c >> 3].rearrange("h s d -> (h s d)").rearrange("(r f) -> r f", f=E)
                sp.dma_start(yrow[:, :, :], rows[ds((c & 7) * SLICE, SLICE), :].rearrange("(t p) f -> p t f", p=P)
                             ).then_inc(y_loaded, DMA)
                if not (isinstance(c, int) and c == 0):
                    sp.wait_ge(xb_ready, c)
                sp.dma_start(xrow[:, :, :], x_tok[ds(c * SLICE, SLICE), :].rearrange("(t p) f -> p t f", p=P)
                             ).then_inc(x_rows_loaded, DMA)

            def store_y(c):
                sp.wait_ge(y_ready, 2 * (c + 1))
                sp.dma_start(out[ds(c * SLICE, SLICE), :].rearrange("(t p) f -> p t f", p=P), y[:, :, :]
                             ).then_inc(y_stored, DMA)

            load_x(0, 0)
            for n, a in w_dram.items():
                sp.dma_start(w[n][:, :, :], a.rearrange("(c p) f -> p c f", p=P)).then_inc(consts_loaded, DMA)
            for i, a in enumerate((mu_r, mu_k)):
                sp.dma_start(mu[:, i, :], a).then_inc(consts_loaded, DMA)
            sp.dma_start(b_col[:, :], b_qk).then_inc(consts_loaded, DMA)
            for dst, a in ((bv_row, bv), (bo_row, bo)):
                sp.dma_start(dst[:, :], a.rearrange("(o f) -> o f", o=1).broadcast_to([P, E])).then_inc(consts_loaded, DMA)
            load_x(1, 1)
            for a in range(2):
                store_v(a)
                store_parts(a)
                load_qkv(a, a)
                if a == 0:
                    sp.wait_ge(k_ready, 1)
                    load_x(2, 0)

            def body(g, i, ahead, scored, begins, ends):
                if ahead:
                    store_v(g + 2)
                    load_x((g + 3) & (SLICES - 1), 1 - i)
                for half in range(2):
                    sp.wait_ge(attn_done, OCTS * g + 2 * half + 3)
                    cols = slice(half * GROUPS // 2, (half + 1) * GROUPS // 2)
                    dst = heads_out[g >> 3, :, ds((g & 7) * SLICE, SLICE), :].rearrange("h (t g) d -> h t g d", t=TOK)
                    sp.dma_start(dst[:, :, cols, :].rearrange("h t g d -> h t (g d)"), attn[:, cols, :]
                                 ).then_inc(attn_stored[half], DMA)
                if begins:
                    for half in range(2):
                        sp.wait_ge(attn_stored[half], (g + 2) * DMA)
                    load_finish(g - LAG + 1)
                if ends:
                    store_y(g - LAG - 1)
                if ahead:
                    store_parts(g + 2)
                    sp.wait_ge(weighed, OCTS * (g + 2))
                    load_qkv(g + 2, i)

            with sp.Fori(0, LAG // 2 - 1) as m:
                for i in range(2):
                    body(2 * m + i, i, True, True, False, False)
            body(LAG - 2, 0, True, True, False, False)
            body(LAG - 1, 1, True, True, True, False)
            body(LAG, 0, True, True, True, False)
            body(LAG + 1, 1, True, True, True, True)
            with sp.Fori(LAG // 2 + 1, SLICES // 2 - 1) as m:
                for i in range(2):
                    body(2 * m + i, i, True, True, True, True)
            body(SLICES - 2, 0, False, True, True, True)
            body(SLICES - 1, 1, False, False, True, True)
            with sp.Fori(SLICES - LAG, SLICES - 1) as c:
                sp.wait_ge(yt_ready, c + 1)
                load_finish(c + 1)
                store_y(c - 1)
            store_y(SLICES - 2)
            store_y(SLICES - 1)
            sp.wait_ge(y_stored, DMA * (SLICES + 1))

        @block.tensor
        def _(pe):
            def rows_by(dst, lhs, name, ready):
                for i in range(2):
                    for c in range(ECH):
                        mm = nc.tensor.matmul(dst[:, i * E:(i + 1) * E], lhs[:, c, i * P:(i + 1) * P], w[name][:, c, :],
                                              start=(c == 0), stop=(c == ECH - 1))
                mm.then_inc(ready, 1)

            def columns_by(dst, rhs, name, first, ready):
                for f in range(ECH):
                    for c in range(ECH):
                        mm = nc.tensor.matmul(dst[:, f * SLICE:(f + 1) * SLICE],
                                              w[name][:, c, first + f * P:first + (f + 1) * P], rhs[:, c, 0:SLICE],
                                              start=(c == 0), stop=(c == ECH - 1))
                mm.then_inc(ready, 1)

            def to_columns(dst, src, ready):
                for ch in range(ECH):
                    for t in range(2):
                        mm = nc.tensor.transpose(dst[:, ch * SLICE + t * P:ch * SLICE + (t + 1) * P],
                                                 src[:, t, ch * P:(ch + 1) * P], ident[:, :])
                mm.then_inc(ready, 1)

            def group_of(t, i, gr):
                return t[i][:, :, :].rearrange("p h (t g) -> p (h t) g", g=GROUPS)[:, :, gr]

            def score_rows(i, o):
                for j in range(OCT):
                    gr = o * OCT + j
                    mm = nc.tensor.matmul(s_ps[o % 2][:, j * P:(j + 1) * P], group_of(qp, i, gr), group_of(kp, i, gr),
                                          start=True, stop=True)
                mm.then_inc(rows_ready, 1)

            def score_columns(i, o):
                for j in range(OCT):
                    gr = o * OCT + j
                    dst = s_ps[o % 2][:, j * P:(j + 1) * P]
                    nc.tensor.matmul(dst, group_of(kp, i, gr), group_of(qp, i, gr), start=True, stop=False)
                    mm = nc.tensor.matmul(dst, select[:, gr, :], max_t[:, :], start=False, stop=True)
                mm.then_inc(cols_ready, 1)

            def weigh(g, i, o):
                pe.wait_ge(exp_done, OCTS * g + o + 1)
                pe.wait_ge(attn_done, OCTS * g + o + 1)
                for n in range(OCT // 4):
                    for j in range(4):
                        mm = nc.tensor.matmul(pv_ps[j * 2 * D:(j + 1) * 2 * D, n * P:(n + 1) * P],
                                              vp[i][:, o * OCT + n * 4 + j, :], probs[o][:, n * 4 + j, :],
                                              start=True, stop=True)
                mm.then_inc(weighed, 1)

            def turn_weighed(g, o):
                pe.wait_ge(weighed_taken, OCTS * g + o + 1)
                for n in range(OCT // 4):
                    mm = nc.tensor.transpose(pv_ps[:, 2 * P + n * P:2 * P + (n + 1) * P], weighed_t[:, n, :], ident[:, :])
                mm.then_inc(pv_ready, 1)

            def turn_maxima(ready):
                mm = nc.tensor.matmul(bank_c[0:PARTS_K, 0:P], max_parts[:, :, :].rearrange("p r g -> p (r g)"),
                                      ident_h[:, :], start=True, stop=True)
                mm.then_inc(ready, 1)

            def score_all_rows(a, i, which):
                for o in which:
                    if o >= 2:
                        pe.wait_ge(max_done, OCTS * a + o - 1)
                    score_rows(i, o)

            pe.wait_ge(consts_loaded, N_CONST_DMAS * DMA)
            pe.wait_ge(scaled, 3)
            for a in range(2):
                pe.wait_ge(x_loaded[a], DMA)
                if a:
                    pe.wait_ge(v_taken, 1)
                rows_by(bank_c, xt[a], "wv", v_ready)
                if a:
                    pe.wait_ge(q_taken, 2)
                columns_by(bank_a, xt[a], "wqk", 0, q_ready)
                if a:
                    pe.wait_ge(k_taken, 2)
                columns_by(bank_b, xt[a], "wqk", E, k_ready)
            pe.wait_ge(tables, N_TABLES)
            pe.wait_ge(identities, 2)
            pe.wait_ge(qk_loaded[0], N_LOAD_DMAS * DMA)
            score_all_rows(0, 0, range(OCTS))

            def key(c, with_q):
                pe.wait_ge(mix_ready, 4 * c + 2)
                if with_q is not None:
                    pe.wait_ge(q_taken, with_q)
                columns_by(bank_a, xk, "wkk", 0, kk_ready)

            def receptance(c, with_k):
                pe.wait_ge(mix_ready, 4 * c + 4)
                if with_k is not None:
                    pe.wait_ge(k_taken, with_k)
                rows_by(bank_b, xr, "wr", r_ready)

            def turn_y(c, dst):
                pe.wait_ge(y_loaded, (c + 1) * DMA)
                to_columns(dst, yrow, yt_ready)

            def project_o(c, dst):
                pe.wait_ge(yt_taken, c + 1)
                rows_by(dst, attn_t, "wo", o_ready)

            def value(c):
                pe.wait_ge(kact_ready, c + 1)
                rows_by(bank_c, k_act, "wvv", vv_ready)

            def turn_x1(c, i):
                pe.wait_ge(x1_ready, 2 * (c + 1))
                to_columns(bank_a, x1[i], xt_ready)

            def body(g, i, ahead, scored, begins, ends):
                c = g - LAG
                projected = g + 2 if ahead else SLICES
                if ends:
                    key(c - 1, 2 * projected)
                    receptance(c - 1, 2 * projected)
                    pe.wait_ge(vv_taken, c)
                pe.wait_ge(maxp_step, 4 * (g + 1))
                pe.wait_ge(v_taken, projected)
                turn_maxima(mt_ready)
                if begins:
                    if ends:
                        pe.wait_ge(kk_taken, c + 1)
                    else:
                        pe.wait_ge(q_taken, 2 * projected)
                    turn_y(c, bank_a)
                pe.wait_ge(mt_taken, g + 1)
                for o in range(2):
                    pe.wait_ge(max_done, OCTS * g + o + 3)
                    score_columns(i, o)
                pe.wait_ge(v_loaded[i], v_count(g, i))
                weigh(g, i, 0)
                if ahead:
                    pe.wait_ge(x_loaded[i], x_count(g, i))
                    rows_by(bank_c, xt[i], "wv", v_ready)
                score_columns(i, 2)
                turn_weighed(g, 0)
                if begins:
                    if ends:
                        pe.wait_ge(r_taken, c)
                    else:
                        pe.wait_ge(k_taken, 2 * projected)
                    project_o(c, bank_b)
                weigh(g, i, 1)
                score_columns(i, 3)
                turn_weighed(g, 1)
                if ends:
                    if ahead:
                        pe.wait_ge(v_taken, g + 3)
                    value(c - 1)
                weigh(g, i, 2)
                if begins:
                    turn_x1(c, i)
                turn_weighed(g, 2)
                if ahead:
                    if begins:
                        pe.wait_ge(xt_taken, c + 1)
                    else:
                        pe.wait_ge(q_taken, 2 * projected)
                    columns_by(bank_a, xt[i], "wqk", 0, q_ready)
                weigh(g, i, 3)
                if scored:
                    pe.wait_ge(qk_loaded[1 - i], qk_count(g, i))
                    score_all_rows(g + 1, 1 - i, range(0, 1))
                turn_weighed(g, 3)
                if scored:
                    score_all_rows(g + 1, 1 - i, range(1, 2))
                if ahead:
                    if begins:
                        pe.wait_ge(z_ready, c + 2)
                    else:
                        pe.wait_ge(k_taken, 2 * projected)
                    columns_by(bank_b, xt[i], "wqk", E, k_ready)
                if scored:
                    score_all_rows(g + 1, 1 - i, range(2, OCTS))

            def x_count(g, i):
                return ((g >> 1) + 2) * DMA

            def v_count(g, i):
                return ((g >> 1) + 1) * DMA

            def qk_count(g, i):
                return ((g + 1 >> 1) + 1) * DMA * N_LOAD_DMAS

            loops(pe, body)

            def last(c, i):
                turn_y(c, s_ps[0][:, 0:512])
                pe.wait_ge(z_ready, c + 1)
                project_o(c, s_ps[0][:, 512:1024])
                key(c - 1, None)
                pe.wait_ge(r_taken, c - 1)
                receptance(c - 1, None)
                pe.wait_ge(kk_taken, c + 1)
                turn_x1(c, i)
                pe.wait_ge(vv_taken, c)
                value(c - 1)

            last_slices(pe, last)
            key(SLICES - 1, None)
            receptance(SLICES - 1, None)
            pe.wait_ge(vv_taken, SLICES)
            value(SLICES - 1)

        @block.scalar
        def _(act):
            def take_projection(a, j, src, ready, taken):
                act.wait_ge(ready, a + 1)
                act.wait_ge(rest_done, 2 * a + j + 1)
                for ch in range(ECH):
                    nc.scalar.activation(full[j][:, ch, :], src[:, ch * SLICE:(ch + 1) * SLICE], ACT.Identity,
                                         bias=b_col[:, j * ECH + ch:j * ECH + ch + 1]).then_inc(taken, 1)
                act.wait_ge(parts_stored, (a + 1) * DMA)
                act.wait_ge(taken, 2 * (a + 1))
                nc.scalar.activation(parts[:, j, 0, :, :], full[j][:, :, :], ACT.Copy).then_inc(hi_done, 1)

            def middle(a, j):
                act.wait_ge(rest_done, 2 * a + j + 3)
                nc.scalar.activation(parts[:, j, 1, :, :], rest[j][:, :, :], ACT.Copy).then_inc(mid_done, 1)

            def take_maxima(a):
                act.wait_ge(mt_ready, a + 1)
                nc.scalar.activation(max_t[:, :], bank_c[0:PARTS_K, 0:P], ACT.Copy).then_inc(mt_taken, 1)

            def take_yt(c, src):
                act.wait_ge(yt_ready, c + 1)
                nc.scalar.activation(flat(attn_t), src[:, 0:2 * E], ACT.Copy).then_inc(yt_taken, 1)

            def take_x1_t(c):
                act.wait_ge(xt_ready, c + 1)
                act.wait_ge(carry_ready, c + 1)
                nc.scalar.activation(x1_t[:, :, 1:1 + SLICE], bank_a[:, :].rearrange("p (c n) -> p c n", c=ECH), ACT.Copy
                                     ).then_inc(xt_taken, 1)

            def take_r(c):
                act.wait_ge(r_ready, c + 1)
                nc.scalar.activation(flat(gate_tanh), bank_b[:, :], ACT.Tanh, scale=0.5).then_inc(r_taken, 1)

            def exp(g, o):
                act.wait_ge(cols_ready, OCTS * g + o + 1)
                act.wait_ge(weighed, OCTS * g + o + 1)
                nc.scalar.activation(flat(probs[o]), s_ps[o % 2][:, :], ACT.Exp).then_inc(exp_done, 1)

            def take_weighed(g, o):
                act.wait_ge(weighed, OCTS * g + o + 1 + OCTS)
                nc.scalar.activation(flat(weighed_t), pv_ps[:, 0:2 * P], ACT.Copy).then_inc(weighed_taken, 1)

            def take_kk(c):
                act.wait_ge(kk_ready, c + 1)
                nc.scalar.activation(flat(k_relu), bank_a[:, :], ACT.Relu).then_inc(kk_taken, 1)

            def mask_k(i):
                own = ident_h[PARTS_K:ROWS, PARTS_K:ROWS].rearrange("r (h t g) -> r h t g", h=1, g=1)
                nc.scalar.activation(kp[i][PARTS_K:ROWS, :, :].rearrange("r h (t g) -> r h t g", t=TOK),
                                     own.broadcast_to([TOK, HEADS, TOK, GROUPS]), ACT.Copy).then_inc(tables, 1)

            act.wait_ge(identities, 2)
            mask_k(0)
            for r in range(3):
                rows = slice(r * GROUPS, (r + 1) * GROUPS)
                own = ident_h[rows, rows].rearrange("r (g o) -> r g o", o=1).broadcast_to([GROUPS, GROUPS, P])
                nc.scalar.activation(select[rows, :, :], own, ACT.Copy, scale=-1.0).then_inc(tables, 1)
            mask_k(1)
            act.wait_ge(scaled, 3)
            for a in range(2):
                take_projection(a, 0, bank_a, q_ready, q_taken)
                take_projection(a, 1, bank_b, k_ready, k_taken)
                middle(a, 0)
                middle(a, 1)

            def body(g, i, ahead, scored, begins, ends):
                c = g - LAG
                if ends:
                    take_kk(c - 1)
                    take_r(c - 1)
                take_maxima(g)
                if begins:
                    take_yt(c, bank_a)
                exp(g, 0)
                exp(g, 1)
                take_weighed(g, 0)
                exp(g, 2)
                take_weighed(g, 1)
                exp(g, 3)
                take_weighed(g, 2)
                if begins:
                    take_x1_t(c)
                take_weighed(g, 3)
                if ahead:
                    take_projection(g + 2, 0, bank_a, q_ready, q_taken)
                    middle(g + 2, 0)
                    take_projection(g + 2, 1, bank_b, k_ready, k_taken)
                    middle(g + 2, 1)

            loops(act, body)

            def last(c, i):
                take_yt(c, s_ps[0])
                take_kk(c - 1)
                take_r(c - 1)
                take_x1_t(c)

            last_slices(act, last)
            take_kk(SLICES - 1)
            take_r(SLICES - 1)

        @block.vector
        def _(dve):
            def take_v(a):
                dve.wait_ge(v_ready, a + 1)
                dve.wait_ge(v_stored, (a + 1) * 2 * DMA)
                bias = bv_row[:, :].rearrange("p (o f) -> p o f", o=1).broadcast_to([P, 2, E])
                nc.vector.tensor_tensor(v_sb[:, :, :], bank_c[:, :].rearrange("p (t f) -> p t f", t=2), bias, ALU.add
                                        ).then_inc(v_taken, 1)

            def lows(a, j):
                dve.wait_ge(mid_done, 2 * a + j + 1)
                nc.vector.tensor_tensor(parts[:, j, 2, :, :], rest[j][:, :, :], parts[:, j, 1, :, :], ALU.subtract
                                        ).then_inc(lo_done, 1)

            def maxes(a, which):
                for o in which:
                    dve.wait_ge(rows_ready, OCTS * a + o + 1)
                    nc.vector.tensor_reduce(maxima[:, o * OCT:(o + 1) * OCT],
                                            s_ps[o % 2][:, :].rearrange("p (g n) -> p g n", g=OCT), AX.X, ALU.max
                                            ).then_inc(max_done, 1)

            def max_split(a):
                dve.wait_ge(max_done, OCTS * (a + 1))
                nc.vector.tensor_copy(max_parts[:, 0, :], maxima[:, :]).then_inc(maxp_step, 1)
                dve.wait_ge(maxp_step, 4 * a + 1)
                nc.vector.tensor_tensor(max_rest[:, :], maxima[:, :], max_parts[:, 0, :], ALU.subtract).then_inc(maxp_step, 1)
                dve.wait_ge(maxp_step, 4 * a + 2)
                nc.vector.tensor_copy(max_parts[:, 1, :], max_rest[:, :]).then_inc(maxp_step, 1)
                dve.wait_ge(maxp_step, 4 * a + 3)
                nc.vector.tensor_tensor(max_parts[:, 2, :], max_rest[:, :], max_parts[:, 1, :], ALU.subtract
                                        ).then_inc(maxp_step, 1)

            def take_attention(g, o):
                cols = slice(o * OCT, (o + 1) * OCT)
                pv = pv_ps[:, 2 * P:4 * P].rearrange("p (g e) -> p g e", e=2 * D)
                dve.wait_ge(pv_ready, OCTS * g + o + 1)
                nc.vector.reciprocal(inv_sum[:, cols], pv[:, :, D]).then_inc(inv_done, 1)
                if o % 2 == 0:
                    dve.wait_ge(attn_stored[o // 2], (g + 1) * DMA)
                dve.wait_ge(inv_done, OCTS * g + o + 1)
                inv = inv_sum[:, cols].rearrange("p (g o) -> p g o", o=1).broadcast_to([P, OCT, D])
                nc.vector.tensor_tensor(attn[:, cols, :], pv[:, :, 0:D], inv, ALU.mult).then_inc(attn_done, 1)

            def moments(src, stats_t, mv, ve, step, c):
                for t in range(2):
                    nc.vector.bn_stats(stats_t[:, t, :], src[:, t, :]).then_inc(step, 1)
                dve.wait_ge(step, c * 5 + 2)
                nc.vector.memset(ve[:, :], 0.0)
                for t in range(2):
                    nc.vector.bn_aggr(mv[:, t, :], stats_t[:, t, :]).then_inc(step, 1)
                dve.wait_ge(step, c * 5 + 4)
                nc.vector.tensor_scalar(ve[:, :], mv[:, :, 1], EPS, None, ALU.add).then_inc(step, 1)

            def take_o(c, src):
                dve.wait_ge(xb_ready, c + 1)
                dve.wait_ge(o_ready, c + 1)
                nc.vector.tensor_tensor(flat(z), src, flat(xb), ALU.add).then_inc(z_ready, 1)
                dve.wait_ge(z_ready, c + 2)
                moments(z, stats, mean_var, var_eps, ln1_step, c)

            def normalise(src, mv, rs, dst, rstd_ready, ready, c):
                dve.wait_ge(rstd_ready, c + 1)
                for t in range(2):
                    nc.vector.tensor_scalar(dst[:, t, :], src[:, t, :], mv[:, t, 0:1], rs[:, t:t + 1],
                                            ALU.subtract, ALU.mult).then_inc(ready, 1)

            def mix(c):
                dve.wait_ge(diff_ready, c + 1)
                for i, dst in ((1, xk), (0, xr)):
                    for ch in range(ECH):
                        nc.vector.scalar_tensor_tensor(out=dst[:, ch, :], in0=diff[:, ch, :], scalar=mu[:, i, ch:ch + 1],
                                                       in1=x1_t[:, ch, 0:SLICE], op0=ALU.mult, op1=ALU.add
                                                       ).then_inc(mix_ready, 1)

            def take_vv(c, i):
                dve.wait_ge(vv_ready, c + 1)
                dve.wait_ge(r_taken, c + 1)
                nc.vector.scalar_tensor_tensor(out=flat(gated), in0=flat(gate_tanh), scalar=1.0, in1=bank_c[:, :],
                                               op0=ALU.add, op1=ALU.mult).then_inc(vv_taken, 1)
                dve.wait_ge(vv_taken, c + 2)
                nc.vector.tensor_tensor(z2[:, :, :], gated[:, :, :], x1[i][:, :, :], ALU.add).then_inc(z2_ready, 1)
                dve.wait_ge(z2_ready, c + 1)
                moments(z2, stats2, mean_var2, var_eps2, ln2_step, c)

            def result(c):
                dve.wait_ge(y_stored, (c + 1) * DMA)
                normalise(z2, mean_var2, rstd2, y, ln2_rstd, y_ready, c)

            def mask_q(i):
                own = ident_h[PARTS_K:ROWS, PARTS_K:ROWS].rearrange("r (h t g) -> r h t g", h=1, g=1)
                nc.vector.tensor_scalar(qp[i][PARTS_K:ROWS, :, :].rearrange("r h (t g) -> r h t g", t=TOK),
                                        own.broadcast_to([TOK, HEADS, TOK, GROUPS]), -MASK, MASK, ALU.mult, ALU.add
                                        ).then_inc(tables, 1)

            dve.wait_ge(identities, 2)
            mask_q(0)
            for i in range(2):
                nc.vector.memset(vp[i][:, :, D:2 * D], 1.0).then_inc(tables, 1)
            dve.wait_ge(consts_loaded, N_CONST_DMAS * DMA)
            nc.vector.tensor_scalar(w["wvv"][:, :, :], w["wvv"][:, :, :], 0.5, None, ALU.mult).then_inc(scaled, 1)
            nc.vector.tensor_scalar(w["wqk"][:, :, 0:E], w["wqk"][:, :, 0:E], SCALE, None, ALU.mult).then_inc(scaled, 1)
            nc.vector.tensor_scalar(b_col[:, 0:ECH], b_col[:, 0:ECH], SCALE, None, ALU.mult).then_inc(scaled, 1)
            for a in range(2):
                take_v(a)
                for j in range(2):
                    lows(a, j)
                if a == 0:
                    mask_q(1)
            maxes(0, range(OCTS))
            max_split(0)

            def body(g, i, ahead, scored, begins, ends):
                c = g - LAG
                if ahead:
                    take_v(g + 2)
                take_attention(g, 0)
                if begins:
                    take_o(c, bank_b[:, :])
                take_attention(g, 1)
                if begins:
                    normalise(z, mean_var, rstd, x1[i], ln1_rstd, x1_ready, c)
                if ends:
                    take_vv(c - 1, 1 - i)
                take_attention(g, 2)
                take_attention(g, 3)
                if scored:
                    maxes(g + 1, range(0, 1))
                    maxes(g + 1, range(1, 2))
                if begins:
                    mix(c)
                if scored:
                    maxes(g + 1, range(2, OCTS))
                    max_split(g + 1)
                if ahead:
                    lows(g + 2, 0)
                    lows(g + 2, 1)
                if ends:
                    result(c - 1)

            loops(dve, body)

            def last(c, i):
                take_o(c, s_ps[0][:, 512:1024])
                normalise(z, mean_var, rstd, x1[i], ln1_rstd, x1_ready, c)
                take_vv(c - 1, 1 - i)
                mix(c)
                result(c - 1)

            last_slices(dve, last)
            take_vv(SLICES - 1, 1)
            result(SLICES - 1)

        @block.gpsimd
        def _(pool):
            def rests(a, j):
                pool.wait_ge(hi_done, 2 * a + j + 1)
                nc.gpsimd.tensor_tensor(rest[j][:, :, :], full[j][:, :, :], parts[:, j, 0, :, :], ALU.subtract
                                        ).then_inc(rest_done, 1)

            def add_bias(c):
                pool.wait_ge(x_rows_loaded, (c + 1) * DMA)
                pool.wait_ge(z_ready, c + 1)
                bias = bo_row[:, :].rearrange("p (o f) -> p o f", o=1).broadcast_to([P, 2, E])
                nc.gpsimd.tensor_tensor(xb[:, :, :], xrow[:, :, :], bias, ALU.add).then_inc(xb_ready, 1)

            def carry_in(c):
                nc.gpsimd.tensor_copy(x1_t[:, :, 0:1], carry[:, :, ds(c & 7, 1)]).then_inc(carry_ready, 1)

            def rsqrt(dst, src, step, ready, c):
                pool.wait_ge(step, (c + 1) * 5)
                nc.gpsimd.tensor_tensor(dst[:, :], src[:, :], minus_half[:, :], ALU.pow).then_inc(ready, 1)

            def differ(c):
                pool.wait_ge(xt_taken, c + 1)
                nc.gpsimd.tensor_tensor(diff[:, :, :], x1_t[:, :, 1:1 + SLICE], x1_t[:, :, 0:SLICE], ALU.subtract
                                        ).then_inc(diff_ready, 1)
                nc.gpsimd.tensor_copy(carry[:, :, ds((c & 7) + 1, 1)], x1_t[:, :, SLICE:SLICE + 1]
                                      ).then_inc(carry_saved, 1)

            def square(c):
                pool.wait_ge(kk_taken, c + 2)
                nc.gpsimd.tensor_tensor(k_act[:, :, :], k_relu[:, :, :], k_relu[:, :, :], ALU.mult).then_inc(kact_ready, 1)

            for n, (s, by) in enumerate(((z_ready, 1), (y_stored, DMA), (attn_done, 1), (attn_stored[0], DMA), (attn_stored[1], DMA),
                                         (rest_done, 2), (vv_taken, 1), (kk_taken, 1), (weighed, OCTS))):
                nc.gpsimd.memset(credit[:, n:n + 1], 0.0).then_inc(s, by)
            nc.gpsimd.memset(minus_half[:, 0:1], -0.5).then_inc(parts_stored, DMA)
            nc.gpsimd.memset(minus_half[:, 1:2], -0.5).then_inc(v_stored, 2 * DMA)

            nc.gpsimd.memset(carry[:, :, :], 0.0).then_inc(zeroed, 1)
            for n, t in enumerate((ident, ident_h)):
                nc.gpsimd.memset(t[:, :], 0.0).then_inc(zeroed, 1)
                pool.wait_ge(zeroed, n + 2)
                nc.gpsimd.affine_select(out=t[:, :], in_=t[:, :], compare_op=ALU.not_equal, fill=1.0, base=0,
                                        pattern=[[-1, P]], channel_multiplier=1).then_inc(identities, 1)
                pool.wait_ge(identities, n + 1)
            for a in range(2):
                for j in range(2):
                    rests(a, j)

            def body(g, i, ahead, scored, begins, ends):
                c = g - LAG
                if ends:
                    square(c - 1)
                if begins:
                    if ends:
                        pool.wait_ge(carry_saved, c)
                    add_bias(c)
                    rsqrt(rstd, var_eps, ln1_step, ln1_rstd, c)
                    carry_in(c)
                    differ(c)
                if ends:
                    rsqrt(rstd2, var_eps2, ln2_step, ln2_rstd, c - 1)
                if ahead:
                    for j in range(2):
                        rests(g + 2, j)

            loops(pool, body)

            def last(c, i):
                pool.wait_ge(carry_saved, c)
                add_bias(c)
                rsqrt(rstd, var_eps, ln1_step, ln1_rstd, c)
                carry_in(c)
                square(c - 1)
                differ(c)
                rsqrt(rstd2, var_eps2, ln2_step, ln2_rstd, c - 1)

            last_slices(pool, last)
            square(SLICES - 1)
            rsqrt(rstd2, var_eps2, ln2_step, ln2_rstd, SLICES - 1)


def kernel(L0_attn_x, L0_attn_Wq, L0_attn_bq, L0_attn_Wk, L0_attn_bk, L0_attn_Wv, L0_attn_bv, L0_attn_Wo, L0_attn_bo,
           L0_ffn_W_r, L0_ffn_W_k, L0_ffn_W_v, L0_ffn_mu_r, L0_ffn_mu_k):
    import numpy as np
    import concourse.bacc as bacc
    from concourse.bass_utils import run_bass_kernel_spmd

    def by_width(a):
        return a.reshape(HEADS, D, -1).swapaxes(0, 1).reshape(a.shape)

    x = np.ascontiguousarray(L0_attn_x).reshape(BATCH * SEQ, E)
    laid = {
        "x_tok": x, "x_t": x.T, "wqk_t": np.concatenate([by_width(L0_attn_Wq), by_width(L0_attn_Wk)]).T, "wv_t": L0_attn_Wv.T,
        "wo_t": L0_attn_Wo.T, "wr_t": L0_ffn_W_r.T, "wkk_t": L0_ffn_W_k.T, "wvv_t": L0_ffn_W_v.T,
        "b_qk": np.concatenate([by_width(L0_attn_bq).reshape(ECH, P), by_width(L0_attn_bk).reshape(ECH, P)]).T, "bv": L0_attn_bv, "bo": L0_attn_bo,
        "mu_r": L0_ffn_mu_r.reshape(ECH, P).T, "mu_k": L0_ffn_mu_k.reshape(ECH, P).T,
    }
    nc = bacc.Bacc("TRN2", target_bir_lowering=False, num_devices=1)
    arrays, args = {}, []
    for name, a in laid.items():
        a = np.ascontiguousarray(a)
        arrays[name] = a
        args.append(nc.dram_tensor(name, a.shape, mybir.dt.from_np(a.dtype), kind="ExternalInput").ap())
    args.append(nc.dram_tensor("y_out", (BATCH * SEQ, E), F32, kind="ExternalOutput").ap())
    build(nc, *args)
    r = run_bass_kernel_spmd(nc, [arrays], core_ids=[0])
    return r.results[0]["y_out"].reshape(BATCH, SEQ, E)
```
